# Optimizing a Trainium2 kernel written in Bass

```python
import numpy as np
import jax
import jax.numpy as jnp

def _softmax(x, axis=-1):
    return jax.nn.softmax(x, axis=axis)
def _gelu(x):
    return jax.nn.gelu(x, approximate=True)
def _silu(x):
    return jax.nn.silu(x)
def _sigmoid(x):
    return jax.nn.sigmoid(x)
def _layernorm(x, axis=-1, eps=1e-5):
    m = jnp.mean(x, axis=axis, keepdims=True)
    v = jnp.var(x, axis=axis, keepdims=True)
    return (x - m) / jnp.sqrt(v + eps)
def _scatter_add(tgt, idx, src, axis=0):
    return tgt.at[idx].add(src)
def _segment_sum(src, seg, n):
    return jax.ops.segment_sum(src, seg, n)

kernel_name = 'mk_conv_preact_d2_conv_nhwc384_e450c2'

def setup_inputs(seed: int = 0):
    np.random.seed(seed)
    _w = jnp.asarray
    def _rec_inputs():
        import jax
        import jax.numpy as jnp
        _gk = jax.random.key(seed)
        x = 0.0001064 + 1 * jax.random.normal(jax.random.fold_in(_gk, 1), (2, 256, 256, 384), jnp.float32)
        return x
    x = _rec_inputs()
    def _L0_conv_setup():
        import jax, jax.numpy as jnp
        import numpy as np
        WINDOW = (1, 5, 20)
        FILL = 1.0

        def box_sum(x, axis, w):
            if w == 1:
                return x
            lo = w // 2
            hi = w - lo - 1
            xm = jnp.moveaxis(x, axis, -1)
            shp = xm.shape
            xr = xm.reshape(-1, 1, shp[-1])
            k = jnp.ones((1, 1, w), x.dtype)
            y = jax.lax.conv_general_dilated(xr, k, window_strides=(1,), padding=[(lo, hi)])
            return jnp.moveaxis(y.reshape(shp), -1, axis)
        key = jax.random.key(seed)
        x = jax.random.normal(key, (2, 256, 256, 384), dtype=jnp.float32)
        return {'x': x}
    _L0_conv_all = _L0_conv_setup()
    _L0_conv_in = {k: v for k, v in _L0_conv_all.items() if k in ()}
    del _L0_conv_all

    def _L1_conv_setup():
        import jax, jax.numpy as jnp
        import numpy as np
        WINDOW = (1, 5, 20)
        FILL = 1.0

        def box_sum(x, axis, w):
            if w == 1:
                return x
            lo = w // 2
            hi = w - lo - 1
            xm = jnp.moveaxis(x, axis, -1)
            shp = xm.shape
            xr = xm.reshape(-1, 1, shp[-1])
            k = jnp.ones((1, 1, w), x.dtype)
            y = jax.lax.conv_general_dilated(xr, k, window_strides=(1,), padding=[(lo, hi)])
            return jnp.moveaxis(y.reshape(shp), -1, axis)
        key = jax.random.key(seed)
        x = jax.random.normal(key, (2, 256, 256, 384), dtype=jnp.float32)
        return {'x': x}
    _L1_conv_all = _L1_conv_setup()
    _L1_conv_in = {k: v for k, v in _L1_conv_all.items() if k in ()}
    del _L1_conv_all

    return {
        "x": x,
    }

def reference(x):
    import jax
    import jax.numpy as jnp
    def _L0_conv_ref(x):
        import jax, jax.numpy as jnp
        import numpy as np
        WINDOW = (1, 5, 20)
        FILL = 1.0

        def box_sum(x, axis, w):
            if w == 1:
                return x
            lo = w // 2
            hi = w - lo - 1
            xm = jnp.moveaxis(x, axis, -1)
            shp = xm.shape
            xr = xm.reshape(-1, 1, shp[-1])
            k = jnp.ones((1, 1, w), x.dtype)
            y = jax.lax.conv_general_dilated(xr, k, window_strides=(1,), padding=[(lo, hi)])
            return jnp.moveaxis(y.reshape(shp), -1, axis)
        w0, w1, w2 = WINDOW
        s = box_sum(box_sum(x, 1, w0), 2, w1)
        num = box_sum(s * s, 3, w2)
        d = box_sum(box_sum(box_sum(x * x, 1, w0), 2, w1), 3, w2)
        c0 = box_sum(jnp.ones((x.shape[1],), x.dtype), 0, w0)
        c1 = box_sum(jnp.ones((x.shape[2],), x.dtype), 0, w1)
        norm = c0[:, None] * c1[None, :]
        denum = d * norm[None, :, :, None]
        return jnp.nan_to_num(num / denum, nan=FILL)

    def _L1_conv_ref(x):
        import jax, jax.numpy as jnp
        import numpy as np
        WINDOW = (1, 5, 20)
        FILL = 1.0

        def box_sum(x, axis, w):
            if w == 1:
                return x
            lo = w // 2
            hi = w - lo - 1
            xm = jnp.moveaxis(x, axis, -1)
            shp = xm.shape
            xr = xm.reshape(-1, 1, shp[-1])
            k = jnp.ones((1, 1, w), x.dtype)
            y = jax.lax.conv_general_dilated(xr, k, window_strides=(1,), padding=[(lo, hi)])
            return jnp.moveaxis(y.reshape(shp), -1, axis)
        w0, w1, w2 = WINDOW
        s = box_sum(box_sum(x, 1, w0), 2, w1)
        num = box_sum(s * s, 3, w2)
        d = box_sum(box_sum(box_sum(x * x, 1, w0), 2, w1), 3, w2)
        c0 = box_sum(jnp.ones((x.shape[1],), x.dtype), 0, w0)
        c1 = box_sum(jnp.ones((x.shape[2],), x.dtype), 0, w1)
        norm = c0[:, None] * c1[None, :]
        denum = d * norm[None, :, :, None]
        return jnp.nan_to_num(num / denum, nan=FILL)

    def _gn(v, G=32, eps=1e-5):
        B_, H_, W_, C_ = v.shape
        g = v.reshape(B_, H_, W_, G, C_ // G)
        m = jnp.mean(g, axis=(1, 2, 4), keepdims=True)
        s = jnp.var(g, axis=(1, 2, 4), keepdims=True)
        return ((g - m) / jnp.sqrt(s + eps)).reshape(v.shape)

    def _ln_c(v, eps=1e-6):
        m = jnp.mean(v, axis=-1, keepdims=True)
        s = jnp.var(v, axis=-1, keepdims=True)
        return (v - m) / jnp.sqrt(s + eps)

    def _ln_t(v, eps=1e-5):
        m = jnp.mean(v, axis=-1, keepdims=True)
        s = jnp.var(v, axis=-1, keepdims=True)
        return (v - m) / jnp.sqrt(s + eps)

    def _to_tokens(v):
        B_, H_, W_, C_ = v.shape
        return v.reshape(B_, H_ * W_, C_)
    def _from_tokens(t, like):
        return t.reshape(like.shape)

    x = x + _L0_conv_ref(_gn(x))
    x = x + _L1_conv_ref(_gn(x))
    return x


_drawn_inputs = setup_inputs


def setup_inputs(seed=0):
    import zlib

    import numpy as np

    out = dict(_drawn_inputs(seed))
    spreads = {}
    factors = {}
    for name, (base, spread) in spreads.items():
        noise = np.random.default_rng([zlib.crc32(name.encode()), seed]).standard_normal(out[name].shape)
        drawn = base * np.exp(spread * noise) if base else spread * noise
        out[name] = jnp.asarray(drawn.astype(out[name].dtype))
    for name, factor in factors.items():
        out[name] = (out[name] * factor).astype(out[name].dtype)
    return out
```

```python
from contextlib import ExitStack

import concourse.bass as bass
from concourse import mybir
from concourse.alu_op_type import AluOpType as ALU

F32 = mybir.dt.float32
ACT = mybir.ActivationFunctionType

P = 128
GROUPS = 32
EPS = 1e-5
W_BOX = 5
C_BOX = 20
C_LO = C_BOX // 2
C_HI = C_BOX - C_LO - 1
TILE_ROWS = 8
PAIRS = TILE_ROWS // 2
BODY = 2 * PAIRS
TINY = 2.0 ** -100
LN_SCALE = 2.0 ** 38
VAR_SCALE = 2.0 ** -40
LN2 = 0.6931471805599453
LN_TABLES = "natural_log_exp_and_others"


def similarity_layers_kernel(nc, x, out):
    B, H, W, C = x.shape
    HALVES = W // P
    KB = C // P
    CG = C // GROUPS
    SEGS = TILE_ROWS * HALVES
    PSEG = 2 * HALVES
    UNITS = 2 * KB
    TILES = H // TILE_ROWS
    NPAIR = H // 2
    LAYERS = 2
    PHASES = [(layer, b) for layer in range(LAYERS) for b in range(B)]
    NP_ = len(PHASES)
    assert W == 2 * P and C == 3 * P and TILES % 4 == 0 and B == 2 and TILES >= 8
    REACH = W_BOX // 2
    WN = P + REACH
    HALF_COL = [0, P - REACH]
    c_span = [(max(0, P * k - C_HI), min(C, P * (k + 1) + C_LO)) for k in range(KB)]

    def tiles_of(t, b):
        return t[b].rearrange("h (j p) c -> p (h j) c", p=P)

    x1 = nc.dram_tensor("first_layer_out", x.shape, F32, kind="Internal").ap()
    source = [x, x1]
    target = [x1, out]

    with ExitStack() as ctx:
        def sb(name, shape, dt=F32):
            return ctx.enter_context(nc.sbuf_tensor(name, shape, dt))

        def sem(name):
            return ctx.enter_context(nc.semaphore(name))

        x_in = [sb(f"x_in{i}", [P, SEGS, C]) for i in range(2)]
        y_out = [sb(f"y_out{i}", [P, SEGS, C]) for i in range(2)]
        stat_tiles = [x_in[0], x_in[1], y_out[0], y_out[1]]
        centred = [sb(f"centred{i}", [P, PSEG, C]) for i in range(2)]
        square = [sb(f"square{i}", [P, PSEG, C]) for i in range(2)]
        sT = [sb(f"sT{i}", [P, KB, 2 * W]) for i in range(2)]
        tT = [sb(f"tT{i}", [P, KB, 2 * W]) for i in range(2)]
        recip = [sb(f"recip{i}", [P, PSEG, C]) for i in range(2)]
        ratio = [sb(f"ratio{i}", [P, PSEG, C]) for i in range(2)]
        group_stats = sb("group_stats", [P, GROUPS, TILES * 6])
        lane_mv = [sb(f"lane_mv{b}", [P, GROUPS, 2]) for b in range(B)]
        stat_tmp = sb("stat_tmp", [P, 8, GROUPS])
        rstd_row = sb("rstd_row", [P, C])
        mean_row = [sb(f"mean_row{i}", [P, C]) for i in range(2)]
        rstd_col = [sb(f"rstd_col{i}", [P, KB]) for i in range(NP_)]
        rvar_col = [sb(f"rvar_col{i}", [P, KB]) for i in range(NP_)]
        band_w = sb("band_w", [P, HALVES, WN])
        band_wc = sb("band_wc", [P, HALVES, WN])
        band_c = [sb(f"band_c{k}", [P, c_span[k][1] - c_span[k][0]]) for k in range(KB)]
        identity = sb("identity", [P, P])
        over_p = sb("over_p", [P, P])
        bias_ln = sb("bias_ln", [P, 1])
        bias_exp = sb("bias_exp", [P, 1])
        bias_var = sb("bias_var", [P, 1])
        bias_rstd = sb("bias_rstd", [P, 1])

        width_ps = [ctx.enter_context(nc.psum_tensor(f"width_ps{i}", [P, 2 * W], F32)) for i in range(3)]
        den_ps = [ctx.enter_context(nc.psum_tensor(f"den_ps{i}", [P, 512], F32)) for i in range(3)]
        num_ps = [ctx.enter_context(nc.psum_tensor(f"num_ps{i}", [P, 512], F32)) for i in range(2)]

        in_landed = [sem(f"in_landed{i}") for i in range(4)]
        out_landed = [sem(f"out_landed{i}") for i in range(2)]
        ones_set = sem("ones_set")
        bands_cut = sem("bands_cut")
        bands_ready = sem("bands_ready")
        constants_ready = sem("constants_ready")
        pool_chain = sem("pool_chain")
        tile_measured = sem("tile_measured")
        rows_centred = sem("rows_centred")
        rows_squared = sem("rows_squared")
        width_done = sem("width_done")
        width_taken = sem("width_taken")
        den_done = sem("den_done")
        num_done = sem("num_done")
        log_done = sem("log_done")
        recip_done = sem("recip_done")
        den_used = sem("den_used")
        num_used = sem("num_used")
        ratio_done = sem("ratio_done")
        rows_out = sem("rows_out")
        stats_done = sem("stats_done")
        dve_chain = sem("dve_chain")
        means_asked = sem("means_asked")
        means_given = sem("means_given")
        log_asked = sem("log_asked")
        log_given = sem("log_given")
        params_ready = sem("params_ready")

        def pairs_before(ph):
            return ph * NPAIR

        def in_phase(ph, p):
            return (ph + 1, p - NPAIR) if isinstance(p, int) and p >= NPAIR else (ph, p)

        def is_opening(ph, p, n):
            return ph == 0 and isinstance(p, int) and p < n

        def looped(eng, n, body, aside=None, at=1):
            body(0, True, False)
            if at > 1:
                with eng.Fori(1, at) as i:
                    body(i, False, False)
            if aside is not None:
                aside()
            if n - 1 > at:
                with eng.Fori(at, n - 1) as i:
                    body(i, False, False)
            body(n - 1, False, True)

        chunk = GROUPS // PAIRS

        with nc.Block() as block:

            @block.sync
            def _(sp):
                for b in range(B):
                    view = tiles_of(x, b)

                    def measure_loads(i, first, last):
                        for s in range(4):
                            if not (first and b == 0):
                                sp.wait_ge(tile_measured, b * TILES + i * 4 + s - 3)
                            sp.dma_start(stat_tiles[s][:], view[:, bass.ds((i * 4 + s) * SEGS, SEGS), :]
                                         ).then_inc(in_landed[s], 16)
                    looped(sp, TILES // 4, measure_loads)
                for s in range(2):
                    sp.wait_ge(tile_measured, B * TILES - 3 + s)
                    sp.dma_start(x_in[s][:], tiles_of(x, 0)[:, s * SEGS:(s + 1) * SEGS, :]
                                 ).then_inc(in_landed[s], 16)
                sp.wait_ge(tile_measured, B * TILES)
                for ph, (layer, b) in enumerate(PHASES):
                    src = tiles_of(source[layer], b)
                    dst = tiles_of(target[layer], b)

                    def move_tiles(i, first, last):
                        for s in range(2):
                            m = i * 2 + s
                            sp.wait_ge(rows_out, pairs_before(ph) + (m + 1) * PAIRS)
                            if not last:
                                sp.dma_start(x_in[s][:], src[:, bass.ds((m + 2) * SEGS, SEGS), :]
                                             ).then_inc(in_landed[s], 16)
                            elif ph + 1 < NP_:
                                nl, nb = PHASES[ph + 1]
                                if nl > 0:
                                    for o in range(2):
                                        sp.wait_ge(out_landed[o], 16 * (TILES // 2) * (nb + 1))
                                sp.dma_start(x_in[s][:], tiles_of(source[nl], nb)[:, s * SEGS:(s + 1) * SEGS, :]
                                             ).then_inc(in_landed[s], 16)
                            sp.dma_start(dst[:, bass.ds(m * SEGS, SEGS), :], y_out[s][:]
                                         ).then_inc(out_landed[s], 16)
                    looped(sp, TILES // 2, move_tiles)
                for s in range(2):
                    sp.wait_ge(out_landed[s], 16 * (TILES // 2) * NP_)

            def loads_before(ph):
                return B * TILES // 4 + ph * (TILES // 2)

            @block.gpsimd
            def _(pool):
                pool.wait_ge(ones_set, 1)
                cuts = 0
                for j in range(HALVES):
                    for band in (band_w, band_wc):
                        off = HALF_COL[j] - P * j
                        nc.gpsimd.affine_select(out=band[:, j, :], in_=band[:, j, :], compare_op=ALU.is_ge, fill=0.0,
                                                base=off + REACH, pattern=[[1, WN]], channel_multiplier=-1
                                                ).then_inc(pool_chain, 1)
                        cuts += 1
                        pool.wait_ge(pool_chain, cuts)
                        nc.gpsimd.affine_select(out=band[:, j, :], in_=band[:, j, :], compare_op=ALU.is_ge, fill=0.0,
                                                base=REACH - off, pattern=[[-1, WN]], channel_multiplier=1
                                                ).then_inc(bands_cut, 1)
                for k in range(KB):
                    lo, hi = c_span[k]
                    n = hi - lo
                    nc.gpsimd.affine_select(out=band_c[k][:], in_=band_c[k][:], compare_op=ALU.is_ge, fill=0.0,
                                            base=lo - P * k + C_HI, pattern=[[1, n]], channel_multiplier=-1
                                            ).then_inc(pool_chain, 1)
                    cuts += 1
                    pool.wait_ge(pool_chain, cuts)
                    nc.gpsimd.affine_select(out=band_c[k][:], in_=band_c[k][:], compare_op=ALU.is_ge, fill=0.0,
                                            base=P * k + C_LO - lo, pattern=[[-1, n]], channel_multiplier=1
                                            ).then_inc(bands_cut, 1)
                nc.gpsimd.affine_select(out=identity[:], in_=identity[:], compare_op=ALU.is_equal, fill=0.0, base=0,
                                        pattern=[[1, P]], channel_multiplier=-1).then_inc(bands_cut, 1)

                def centre(ph, p, i, e):
                    slot, g = e // PAIRS, e % PAIRS
                    if isinstance(p, int) and p == 0:
                        pool.wait_ge(params_ready, ph + 1)
                    if g == 0:
                        pool.wait_ge(in_landed[slot], (loads_before(ph) + i + 1) * 16)
                    if not (ph == 0 and isinstance(p, int) and p < 2):
                        pool.wait_ge(width_done, (ph * NPAIR + p - 1) * UNITS)
                    nc.gpsimd.tensor_tensor(centred[e % 2][:], x_in[slot][:, g * PSEG:(g + 1) * PSEG, :],
                                            mean_row[ph % 2][:].unsqueeze(1).to_broadcast([P, PSEG, C]),
                                            ALU.subtract).then_inc(rows_centred, 1)

                def add_ratio(ph, p, i, e):
                    slot, g = e // PAIRS, e % PAIRS
                    first = isinstance(i, int) and i == 0
                    if g == 0:
                        if not (first and ph == 0):
                            pool.wait_ge(out_landed[slot], (ph * (TILES // 2) + i) * 16)
                        if (PHASES[ph][0] == 0 and not (first and ph == 0)) or (first and ph == B):
                            pool.wait_ge(stats_done, (ph * TILES + i * 2 + slot - 1) * PAIRS)
                    pool.wait_ge(ratio_done, ph * NPAIR + p + 1)
                    nc.gpsimd.tensor_tensor(y_out[slot][:, g * PSEG:(g + 1) * PSEG, :],
                                            x_in[slot][:, g * PSEG:(g + 1) * PSEG, :],
                                            ratio[e % 2][:], ALU.subtract).then_inc(rows_out, 1)

                centre(0, 0, 0, 0)
                centre(0, 1, 0, 1)
                for ph in range(NP_):
                    def tiles(i, first, last):
                        for e in range(BODY):
                            p = i * BODY + e
                            if last and e + 2 >= BODY:
                                if ph + 1 < NP_:
                                    centre(ph + 1, e + 2 - BODY, 0, e + 2 - BODY)
                            else:
                                centre(ph, p + 2, i + (e + 2) // BODY, (e + 2) % BODY)
                            if e > 0:
                                add_ratio(ph, p - 1, i, e - 1)
                            elif not first:
                                add_ratio(ph, p - 1, i - 1, BODY - 1)
                            elif ph > 0:
                                add_ratio(ph - 1, NPAIR - 1, TILES // 2 - 1, BODY - 1)
                    looped(pool, NPAIR // BODY, tiles)
                add_ratio(NP_ - 1, NPAIR - 1, TILES // 2 - 1, BODY - 1)

            @block.scalar
            def _(act):
                act.preload_act_table_set(LN_TABLES)
                act.wait_ge(constants_ready, 1)

                def finish_logs(ph):
                    n = ph + 1
                    act.wait_ge(log_asked, n)
                    nc.scalar.activation(stat_tmp[:, 3, :], stat_tmp[:, 2, :], ACT.Ln, bias=bias_var[:],
                                         scale=VAR_SCALE).then_inc(log_given, 1)
                    act.wait_ge(log_given, 2 * n - 1)
                    nc.scalar.activation(stat_tmp[:, 4, :], stat_tmp[:, 3, :], ACT.Exp, bias=bias_rstd[:],
                                         scale=-0.5).then_inc(log_given, 1)

                def squares(ph, p, par, half):
                    if half == 0:
                        act.wait_ge(rows_centred, ph * NPAIR + p + 1)
                        if not is_opening(ph, p, 2):
                            act.wait_ge(width_done, (ph * NPAIR + p - 1) * UNITS)
                    h = slice(half * 2, half * 2 + 2)
                    nc.scalar.activation(square[par][:, h, :], centred[par][:, h, :], ACT.Square
                                         ).then_inc(rows_squared, 1)

                def take(ph, p, par, k, is_t):
                    u = 2 * k + is_t
                    if u == 0:
                        if isinstance(p, int) and p == 0:
                            act.wait_ge(params_ready, ph + 1)
                        if not is_opening(ph, p, 2):
                            act.wait_ge(num_done, (ph * NPAIR + p - 1) * PSEG)
                    act.wait_ge(width_done, (ph * NPAIR + p) * UNITS + u + 1)
                    src = width_ps[u % 3][:]
                    if is_t:
                        nc.scalar.activation(tT[par][:, k, :], src, ACT.Copy, scale=rvar_col[ph][:, k:k + 1]
                                             ).then_inc(width_taken, 1)
                    else:
                        nc.scalar.activation(sT[par][:, k, :], src, ACT.Square, scale=rstd_col[ph][:, k:k + 1]
                                             ).then_inc(width_taken, 1)

                def invert(ph, p, par, i):
                    base = ph * NPAIR
                    if i == 0 and not is_opening(ph, p, 2):
                        act.wait_ge(ratio_done, base + p - 1)
                    act.wait_ge(den_done, (base + p) * PSEG + i + 1)
                    nc.scalar.activation(recip[par][:, i, :], den_ps[i % 3][:, 0:C], ACT.Ln, bias=bias_ln[:],
                                         scale=LN_SCALE).then_inc(log_done, 1)
                    act.wait_ge(log_done, (base + p) * PSEG + i + 1)
                    nc.scalar.activation(recip[par][:, i, :], recip[par][:, i, :], ACT.Exp, bias=bias_exp[:],
                                         scale=-1.0).then_inc(recip_done, 1)

                def step(ph, p, par):
                    (ph1, p1), (ph2, p2) = in_phase(ph, p + 1), in_phase(ph, p + 2)
                    for what in ("S0", "L0", "T0", "L1", "S1", "Q0", "T1", "L2", "Q1", "S2", "T2", "L3"):
                        n = int(what[1])
                        if what[0] == "L":
                            invert(ph, p, par, n)
                        elif what[0] == "Q":
                            if ph2 < NP_:
                                squares(ph2, p2, par, n)
                        elif ph1 < NP_:
                            take(ph1, p1, 1 - par, n, int(what[0] == "T"))

                finish_logs(0)
                for p in range(2):
                    for half in range(2):
                        squares(0, p, p, half)
                for k in range(KB):
                    take(0, 0, 0, k, 0)
                    take(0, 0, 0, k, 1)
                for ph in range(NP_):
                    def pairs(i, first, last):
                        step(ph, i * 2, 0)
                        step(ph, i * 2 + 1, 1)
                    looped(act, NPAIR // 2, pairs, (lambda: finish_logs(ph + 1)) if ph + 1 < NP_ else None, BODY // 2)

            @block.tensor
            def _(pe):
                pe.wait_ge(bands_ready, 1)
                pe.wait_ge(constants_ready, 1)

                def finish_sums(ph):
                    n = 3 * ph
                    pe.wait_ge(means_asked, n + 1)
                    nc.tensor.matmul(num_ps[0][:, 0:GROUPS], over_p[:], stat_tmp[:, 0, :], start=True, stop=True
                                     ).then_inc(means_given, 1)
                    pe.wait_ge(means_asked, n + 2)
                    nc.tensor.matmul(num_ps[1][:, 0:GROUPS], over_p[:], stat_tmp[:, 1, :], start=True, stop=True
                                     ).then_inc(means_given, 1)
                    pe.wait_ge(means_asked, n + 3)
                    for k in range(KB):
                        last = nc.tensor.transpose(den_ps[0][:, P * k:P * (k + 1)], rstd_row[:, P * k:P * (k + 1)],
                                                   identity[:])
                    last.then_inc(means_given, 1)
                    pe.wait_ge(params_ready, ph + 1)

                def width_unit(ph, p, par, k, is_t):
                    u = 2 * k + is_t
                    if u == 0:
                        pe.wait_ge(rows_centred, ph * NPAIR + p + 1)
                    if u == 1:
                        pe.wait_ge(rows_squared, (ph * NPAIR + p + 1) * 2)
                    if not (is_opening(ph, p, 1) and u < 3):
                        pe.wait_ge(width_taken, (ph * NPAIR + p) * UNITS + u - 2)
                    data = square[par] if is_t else centred[par]
                    band = band_wc if is_t else band_w
                    bank = width_ps[u % 3]
                    for r in range(2):
                        for j in range(HALVES):
                            at = r * W + HALF_COL[j]
                            last = nc.tensor.matmul(bank[:, at:at + WN], data[:, r * 2 + j, P * k:P * (k + 1)],
                                                    band[:, j, :], start=(r == 0 and j == 0),
                                                    stop=(r == 1 and j == 1), skip_group_check=True)
                    last.then_inc(width_done, 1)

                def channel_unit(ph, p, par, i, is_num):
                    seg = (ph * NPAIR + p) * PSEG + i
                    if i == 0 and not is_num:
                        pe.wait_ge(width_taken, (ph * NPAIR + p + 1) * UNITS)
                    if is_num:
                        bank, data = num_ps[i % 2], sT[par]
                        if not (is_opening(ph, p, 1) and i < 2):
                            pe.wait_ge(num_used, seg - 1)
                    else:
                        bank, data = den_ps[i % 3], tT[par]
                        if not (is_opening(ph, p, 1) and i < 3):
                            pe.wait_ge(den_used, seg if i == 0 else seg - 2 if i == 3 else seg - 3)
                    at = (i // 2) * W + (i % 2) * P
                    for k in range(KB):
                        lo, hi = c_span[k]
                        last = nc.tensor.matmul(bank[:, lo:hi], data[:, k, at:at + P], band_c[k][:],
                                                start=(k == 0), stop=(k == KB - 1), skip_group_check=True)
                    last.then_inc(num_done if is_num else den_done, 1)

                def step(ph, p, par):
                    ph1, p1 = in_phase(ph, p + 1)
                    for what in ("S0", "D0", "T0", "D1", "S1", "N0", "T1", "D2", "S2", "N1", "T2", "D3", "N2", "N3"):
                        n = int(what[1])
                        if what[0] in "DN":
                            channel_unit(ph, p, par, n, what[0] == "N")
                        elif ph1 < NP_:
                            width_unit(ph1, p1, 1 - par, n, int(what[0] == "T"))

                finish_sums(0)
                for k in range(KB):
                    width_unit(0, 0, 0, k, 0)
                    width_unit(0, 0, 0, k, 1)
                for ph in range(NP_):
                    def pairs(i, first, last):
                        step(ph, i * 2, 0)
                        step(ph, i * 2 + 1, 1)
                    looped(pe, NPAIR // 2, pairs, (lambda: finish_sums(ph + 1)) if ph + 1 < NP_ else None, BODY // 2)

            @block.vector
            def _(dve):
                links = [0]

                def link(instruction):
                    links[0] += 1
                    instruction.then_inc(dve_chain, 1)
                    dve.wait_ge(dve_chain, links[0])

                for j in range(HALVES):
                    nc.vector.memset(band_w[:, j, :], 1.0)
                    nc.vector.memset(band_wc[:, j, :], float(W_BOX))
                for k in range(KB):
                    nc.vector.memset(band_c[k][:], 1.0)
                nc.vector.memset(identity[:], 1.0).then_inc(ones_set, 1)
                nc.vector.memset(over_p[:], 1.0 / P)
                nc.vector.memset(bias_ln[:], TINY * LN_SCALE)
                nc.vector.memset(bias_exp[:], LN2 * 38)
                nc.vector.memset(bias_var[:], EPS * VAR_SCALE)
                nc.vector.memset(bias_rstd[:], -LN2 * 20).then_inc(constants_ready, 1)

                def measure(tile, groups, index):
                    for g in groups:
                        last = nc.vector.bn_stats(group_stats[:, g, bass.ds(index * 6, 6)],
                                                  tile[:, :, CG * g:CG * (g + 1)])
                    return last

                def lane_totals(b, groups):
                    for g in groups:
                        last = nc.vector.bn_aggr(lane_mv[b][:, g, :], group_stats[:, g, :])
                    link(last)

                for b in range(B):
                    def measure_tiles(i, first, last):
                        for s in range(4):
                            dve.wait_ge(in_landed[s], (b * (TILES // 4) + i + 1) * 16)
                            measure(stat_tiles[s], range(GROUPS), i * 4 + s).then_inc(tile_measured, 1)
                    looped(dve, TILES // 4, measure_tiles)
                    dve.wait_ge(tile_measured, (b + 1) * TILES)
                    lane_totals(b, range(GROUPS))

                dve.wait_ge(bands_cut, 2 * HALVES + KB + 1)
                for d in range(REACH):
                    for j, col in ((0, d), (1, WN - 1 - d)):
                        last = nc.vector.tensor_scalar(band_wc[:, j, col:col + 1], band_w[:, j, col:col + 1],
                                                       float(REACH + 1 + d), None, ALU.mult)
                last.then_inc(bands_ready, 1)

                def finish(ph):
                    b = PHASES[ph][1]
                    asked, logs = 3 * ph, ph + 1
                    mean_l, var_l = lane_mv[b][:, :, 0], lane_mv[b][:, :, 1]
                    nc.vector.tensor_copy(stat_tmp[:, 0, :], mean_l).then_inc(means_asked, 1)
                    dve.wait_ge(means_given, asked + 1)
                    mean = num_ps[0][:, 0:GROUPS]
                    link(nc.vector.tensor_tensor(stat_tmp[:, 5, :], mean_l, mean, ALU.subtract))
                    link(nc.vector.tensor_tensor(stat_tmp[:, 6, :], stat_tmp[:, 5, :], stat_tmp[:, 5, :], ALU.mult))
                    nc.vector.tensor_tensor(stat_tmp[:, 1, :], stat_tmp[:, 6, :], var_l, ALU.add
                                            ).then_inc(means_asked, 1)
                    nc.vector.tensor_copy(mean_row[ph % 2][:].rearrange("p (g c) -> p g c", c=CG),
                                          mean.unsqueeze(2).to_broadcast([P, GROUPS, CG]))
                    dve.wait_ge(means_given, asked + 2)
                    nc.vector.tensor_copy(stat_tmp[:, 2, :], num_ps[1][:, 0:GROUPS]).then_inc(log_asked, 1)
                    dve.wait_ge(log_asked, logs)
                    link(nc.vector.tensor_scalar(stat_tmp[:, 7, :], stat_tmp[:, 2, :], EPS, None, ALU.add))
                    dve.wait_ge(log_given, 2 * logs)
                    link(nc.vector.tensor_tensor(stat_tmp[:, 5, :], stat_tmp[:, 4, :], stat_tmp[:, 4, :], ALU.mult))
                    link(nc.vector.tensor_tensor(stat_tmp[:, 6, :], stat_tmp[:, 5, :], stat_tmp[:, 7, :], ALU.mult))
                    link(nc.vector.tensor_scalar(stat_tmp[:, 5, :], stat_tmp[:, 6, :], -0.5, 1.5, ALU.mult, ALU.add))
                    link(nc.vector.tensor_tensor(stat_tmp[:, 6, :], stat_tmp[:, 5, :], stat_tmp[:, 4, :], ALU.mult))
                    nc.vector.tensor_copy(rstd_row[:].rearrange("p (g c) -> p g c", c=CG),
                                          stat_tmp[:, 6, :].unsqueeze(2).to_broadcast([P, GROUPS, CG])
                                          ).then_inc(means_asked, 1)
                    dve.wait_ge(means_given, asked + 3)
                    link(nc.vector.tensor_copy(rstd_col[ph][:], den_ps[0][:, 0:C].rearrange(
                        "p (k n) -> p k n", n=P)[:, :, 0]))
                    nc.vector.tensor_tensor(rvar_col[ph][:], rstd_col[ph][:], rstd_col[ph][:], ALU.mult
                                            ).then_inc(params_ready, 1)
                    dve.wait_ge(params_ready, ph + 1)

                def divide(ph, p, par):
                    base = ph * NPAIR
                    for what in ("a0", "a1", "w0", "a2", "w1", "a3", "w2", "w3"):
                        i = int(what[1])
                        seg = (base + p) * PSEG + i
                        if what[0] == "a":
                            dve.wait_ge(recip_done, seg + 1)
                            if i == 0 and not is_opening(ph, p, 2):
                                dve.wait_ge(rows_out, base + p - 1)
                            nc.vector.scalar_tensor_tensor(ratio[par][:, i, :], den_ps[i % 3][:, 0:C], TINY,
                                                           recip[par][:, i, :], ALU.add, ALU.mult
                                                           ).then_inc(den_used, 1)
                        else:
                            dve.wait_ge(num_done, seg + 1)
                            nc.vector.scalar_tensor_tensor(recip[par][:, i, :], num_ps[i % 2][:, 0:C], TINY,
                                                           recip[par][:, i, :], ALU.add, ALU.mult
                                                           ).then_inc(num_used, 1)
                    dve.wait_ge(num_used, (base + p + 1) * PSEG)
                    dve.wait_ge(den_used, (base + p + 1) * PSEG)
                    nc.vector.scalar_tensor_tensor(ratio[par][:], ratio[par][:], 2.0, recip[par][:],
                                                   ALU.subtract, ALU.mult).then_inc(ratio_done, 1)

                finish(0)
                for ph, (layer, b) in enumerate(PHASES):
                    def tiles(i, first, last):
                        for e in range(BODY):
                            divide(ph, i * BODY + e, e % 2)
                            q = e % PAIRS
                            quarter = range(q * chunk, (q + 1) * chunk)
                            slot = (e // PAIRS + 1) % 2
                            if not (first and e < PAIRS):
                                if layer == 0:
                                    m = i * 2 + e // PAIRS - 1
                                    if q == 0:
                                        dve.wait_ge(rows_out, ph * NPAIR + (m + 1) * PAIRS)
                                    measure(y_out[slot], quarter, m).then_inc(stats_done, 1)
                            elif 0 < ph <= B:
                                if q == 0:
                                    dve.wait_ge(rows_out, ph * NPAIR)
                                measure(y_out[slot], quarter, TILES - 1).then_inc(stats_done, 1)
                                dve.wait_ge(stats_done, (ph - 1) * NPAIR + NPAIR - PAIRS + q + 1)
                                lane_totals(PHASES[ph - 1][1], quarter)
                    looped(dve, NPAIR // BODY, tiles, (lambda: finish(ph + 1)) if ph + 1 < NP_ else None, 1)


def kernel(x):
    import numpy as np
    import concourse.bacc as bacc
    from concourse.bass_utils import run_bass_kernel_spmd

    nc = bacc.Bacc("TRN2", target_bir_lowering=False, num_devices=1)
    a = np.ascontiguousarray(x)
    xin = nc.dram_tensor("in_x_dram", a.shape, mybir.dt.from_np(a.dtype), kind="ExternalInput").ap()
    out = nc.dram_tensor("out_0_dram", a.shape, mybir.dt.from_np(a.dtype), kind="ExternalOutput").ap()
    similarity_layers_kernel(nc, xin, out)
    r = run_bass_kernel_spmd(nc, [{"in_x_dram": a}], core_ids=[0])
    return r.results[0]["out_0_dram"]
```

```python
from contextlib import ExitStack

import concourse.bass as bass
from concourse import mybir
from concourse.alu_op_type import AluOpType as ALU

F32 = mybir.dt.float32
ACT = mybir.ActivationFunctionType

P = 128
GROUPS = 32
EPS = 1e-5
W_BOX = 5
C_BOX = 20
C_LO = C_BOX // 2
C_HI = C_BOX - C_LO - 1
TILE_ROWS = 8
PAIRS = TILE_ROWS // 2
BODY = 2 * PAIRS
TINY = 2.0 ** -100
LN_SCALE = 2.0 ** 38
VAR_SCALE = 2.0 ** -40
LN2 = 0.6931471805599453
LN_TABLES = "natural_log_exp_and_others"


def similarity_layers_kernel(nc, x, out):
    B, H, W, C = x.shape
    HALVES = W // P
    KB = C // P
    CG = C // GROUPS
    SEGS = TILE_ROWS * HALVES
    PSEG = 2 * HALVES
    UNITS = 2 * KB
    TILES = H // TILE_ROWS
    NPAIR = H // 2
    LAYERS = 2
    PHASES = [(layer, b) for layer in range(LAYERS) for b in range(B)]
    NP_ = len(PHASES)
    assert W == 2 * P and C == 3 * P and TILES % 4 == 0 and B == 2 and TILES >= 8
    SPLIT = TILES // 2
    MID = SPLIT // 2
    UPFRONT = 4
    BESIDE = TILES - UPFRONT
    BESIDE_SPLIT = (SPLIT - UPFRONT) // 2
    BESIDE_END = BESIDE // 2
    REACH = W_BOX // 2
    WN = P + REACH
    HALF_COL = [0, P - REACH]
    c_span = [(max(0, P * k - C_HI), min(C, P * (k + 1) + C_LO)) for k in range(KB)]

    def tiles_of(t, b):
        return t[b].rearrange("h (j p) c -> p (h j) c", p=P)

    x1 = nc.dram_tensor("first_layer_out", x.shape, F32, kind="Internal").ap()
    source = [x, x1]
    target = [x1, out]

    with ExitStack() as ctx:
        def sb(name, shape, dt=F32):
            return ctx.enter_context(nc.sbuf_tensor(name, shape, dt))

        def sem(name):
            return ctx.enter_context(nc.semaphore(name))

        x_in = [sb(f"x_in{i}", [P, SEGS, C]) for i in range(2)]
        y_out = [sb(f"y_out{i}", [P, SEGS, C]) for i in range(2)]
        stat_tiles = [x_in[0], x_in[1], y_out[0], y_out[1]]
        centred = [sb(f"centred{i}", [P, PSEG, C]) for i in range(2)]
        square = [sb(f"square{i}", [P, PSEG, C]) for i in range(2)]
        sT = [sb(f"sT{i}", [P, KB, 2 * W]) for i in range(2)]
        tT = [sb(f"tT{i}", [P, KB, 2 * W]) for i in range(2)]
        recip = [sb(f"recip{i}", [P, PSEG, C]) for i in range(2)]
        newton = sb("newton", [P, PSEG, C])
        beside = sb("beside", [P, SEGS, C])
        out_stats = sb("out_stats", [P, GROUPS, SPLIT * 6])
        beside_stats = sb("beside_stats", [P, GROUPS, SPLIT * 6])
        lane_mv = [sb(f"lane_mv{b}", [P, 2, GROUPS, 2]) for b in range(B)]
        stat_tmp = sb("stat_tmp", [P, 5, GROUPS])
        stat_two = sb("stat_two", [P, 3, 2, GROUPS])
        rstd_row = sb("rstd_row", [P, C])
        mean_row = [sb(f"mean_row{i}", [P, C]) for i in range(2)]
        rstd_col = [sb(f"rstd_col{i}", [P, KB]) for i in range(NP_)]
        rvar_col = [sb(f"rvar_col{i}", [P, KB]) for i in range(NP_)]
        band_w = sb("band_w", [P, HALVES, WN])
        band_wc = sb("band_wc", [P, HALVES, WN])
        band_c = [sb(f"band_c{k}", [P, c_span[k][1] - c_span[k][0]]) for k in range(KB)]
        identity = sb("identity", [P, P])
        over_p = sb("over_p", [P, P])
        bias_ln = sb("bias_ln", [P, 1])
        bias_exp = sb("bias_exp", [P, 1])
        bias_var = sb("bias_var", [P, 1])
        bias_rstd = sb("bias_rstd", [P, 1])

        width_ps = [ctx.enter_context(nc.psum_tensor(f"width_ps{i}", [P, 2 * W], F32)) for i in range(3)]
        den_ps = [ctx.enter_context(nc.psum_tensor(f"den_ps{i}", [P, 512], F32)) for i in range(3)]
        num_ps = [ctx.enter_context(nc.psum_tensor(f"num_ps{i}", [P, 512], F32)) for i in range(2)]

        in_landed = [sem(f"in_landed{i}") for i in range(4)]
        out_landed = [sem(f"out_landed{i}") for i in range(2)]
        ones_set = sem("ones_set")
        bands_cut = sem("bands_cut")
        bands_ready = sem("bands_ready")
        constants_ready = sem("constants_ready")
        pool_chain = sem("pool_chain")
        beside_landed = sem("beside_landed")
        beside_done = sem("beside_done")
        tile_measured = sem("tile_measured")
        rows_centred = sem("rows_centred")
        rows_squared = sem("rows_squared")
        width_done = sem("width_done")
        width_taken = sem("width_taken")
        den_done = sem("den_done")
        num_done = sem("num_done")
        log_done = sem("log_done")
        recip_done = sem("recip_done")
        den_used = sem("den_used")
        num_used = sem("num_used")
        ratio_done = sem("ratio_done")
        rows_out = sem("rows_out")
        stats_done = sem("stats_done")
        dve_chain = sem("dve_chain")
        means_asked = sem("means_asked")
        means_given = sem("means_given")
        log_asked = sem("log_asked")
        log_given = sem("log_given")
        params_ready = sem("params_ready")

        def pairs_before(ph):
            return ph * NPAIR

        def in_phase(ph, p):
            return (ph + 1, p - NPAIR) if isinstance(p, int) and p >= NPAIR else (ph, p)

        def is_opening(ph, p, n):
            return ph == 0 and isinstance(p, int) and p < n

        def looped(eng, n, body, peeled, cuts=()):
            calls = {at: call for at, call in cuts}
            starts = sorted({0, n} | set(calls) | {p for p in peeled} | {p + 1 for p in peeled if p + 1 < n})
            for lo, hi in zip(starts, starts[1:]):
                if calls.get(lo) is not None:
                    calls[lo]()
                if lo in peeled:
                    body(lo, lo)
                elif hi > lo:
                    with eng.Fori(lo, hi) as i:
                        body(i, lo)

        def finish_pair(ph):
            return BESIDE_END * BODY if ph == 0 else BODY

        chunk = GROUPS // PAIRS

        with nc.Block() as block:

            @block.sync
            def _(sp):
                view = tiles_of(x, 0)

                def measure_loads(i, lo):
                    for s in range(4):
                        if lo > 0:
                            sp.wait_ge(tile_measured, i * 4 + s - 3)
                        sp.dma_start(stat_tiles[s][:], view[:, bass.ds((i * 4 + s) * SEGS, SEGS), :]
                                     ).then_inc(in_landed[s], 16)
                looped(sp, TILES // 4, measure_loads, [0])
                for s in range(UPFRONT):
                    sp.wait_ge(tile_measured, TILES + s - 3)
                    sp.dma_start(stat_tiles[s][:], tiles_of(x, 1)[:, s * SEGS:(s + 1) * SEGS, :]
                                 ).then_inc(in_landed[s], 16)
                for s in range(2):
                    sp.wait_ge(tile_measured, TILES + UPFRONT - 3 + s)
                    sp.dma_start(x_in[s][:], tiles_of(x, 0)[:, s * SEGS:(s + 1) * SEGS, :]
                                 ).then_inc(in_landed[s], 16)

                def load_beside(n):
                    sp.dma_start(beside[:], tiles_of(x, 1)[:, bass.ds((UPFRONT + n) * SEGS, SEGS), :]
                                 ).then_inc(beside_landed, 16)
                load_beside(0)
                sp.wait_ge(beside_done, 1)
                load_beside(1)
                for ph, (layer, b) in enumerate(PHASES):
                    src = tiles_of(source[layer], b)
                    dst = tiles_of(target[layer], b)
                    bodies = TILES // 2

                    def move_tiles(i, lo):
                        last = lo == bodies - 1
                        for s in range(2):
                            m = i * 2 + s
                            sp.wait_ge(rows_out, pairs_before(ph) + (m + 1) * PAIRS)
                            if not last:
                                sp.dma_start(x_in[s][:], src[:, bass.ds((m + 2) * SEGS, SEGS), :]
                                             ).then_inc(in_landed[s], 16)
                            elif ph + 1 < NP_:
                                nl, nb = PHASES[ph + 1]
                                if nl > 0:
                                    for o in range(2):
                                        sp.wait_ge(out_landed[o], 16 * (TILES // 2) * (nb + 1))
                                sp.dma_start(x_in[s][:], tiles_of(source[nl], nb)[:, s * SEGS:(s + 1) * SEGS, :]
                                             ).then_inc(in_landed[s], 16)
                            sp.dma_start(dst[:, bass.ds(m * SEGS, SEGS), :], y_out[s][:]
                                         ).then_inc(out_landed[s], 16)
                            if ph == 0 and lo < BESIDE_END - 1:
                                sp.wait_ge(beside_done, m + 2)
                                load_beside(m + 2)
                    looped(sp, bodies, move_tiles, [bodies - 1], [(BESIDE_END - 1, None)] if ph == 0 else [])
                for s in range(2):
                    sp.wait_ge(out_landed[s], 16 * (TILES // 2) * NP_)

            def loads_before(ph):
                return (TILES + UPFRONT) // 4 + ph * (TILES // 2)

            @block.gpsimd
            def _(pool):
                pool.wait_ge(ones_set, 1)
                cuts = 0
                for j in range(HALVES):
                    for band in (band_w, band_wc):
                        off = HALF_COL[j] - P * j
                        nc.gpsimd.affine_select(out=band[:, j, :], in_=band[:, j, :], compare_op=ALU.is_ge, fill=0.0,
                                                base=off + REACH, pattern=[[1, WN]], channel_multiplier=-1
                                                ).then_inc(pool_chain, 1)
                        cuts += 1
                        pool.wait_ge(pool_chain, cuts)
                        nc.gpsimd.affine_select(out=band[:, j, :], in_=band[:, j, :], compare_op=ALU.is_ge, fill=0.0,
                                                base=REACH - off, pattern=[[-1, WN]], channel_multiplier=1
                                                ).then_inc(bands_cut, 1)
                for k in range(KB):
                    lo, hi = c_span[k]
                    n = hi - lo
                    nc.gpsimd.affine_select(out=band_c[k][:], in_=band_c[k][:], compare_op=ALU.is_ge, fill=0.0,
                                            base=lo - P * k + C_HI, pattern=[[1, n]], channel_multiplier=-1
                                            ).then_inc(pool_chain, 1)
                    cuts += 1
                    pool.wait_ge(pool_chain, cuts)
                    nc.gpsimd.affine_select(out=band_c[k][:], in_=band_c[k][:], compare_op=ALU.is_ge, fill=0.0,
                                            base=P * k + C_LO - lo, pattern=[[-1, n]], channel_multiplier=1
                                            ).then_inc(bands_cut, 1)
                nc.gpsimd.affine_select(out=identity[:], in_=identity[:], compare_op=ALU.is_equal, fill=0.0, base=0,
                                        pattern=[[1, P]], channel_multiplier=-1).then_inc(bands_cut, 1)

                def centre(ph, p, i, e):
                    slot, g = e // PAIRS, e % PAIRS
                    if isinstance(p, int) and p == 0:
                        pool.wait_ge(params_ready, ph + 1)
                    if g == 0:
                        pool.wait_ge(in_landed[slot], (loads_before(ph) + i + 1) * 16)
                    if not (ph == 0 and isinstance(p, int) and p < 2):
                        pool.wait_ge(width_done, (ph * NPAIR + p - 1) * UNITS)
                    nc.gpsimd.tensor_tensor(centred[e % 2][:], x_in[slot][:, g * PSEG:(g + 1) * PSEG, :],
                                            mean_row[ph % 2][:].unsqueeze(1).to_broadcast([P, PSEG, C]),
                                            ALU.subtract).then_inc(rows_centred, 1)

                def add_ratio(ph, p, i, e):
                    slot, g = e // PAIRS, e % PAIRS
                    pool.wait_ge(ratio_done, ph * NPAIR + p + 1)
                    nc.gpsimd.tensor_tensor(y_out[slot][:, g * PSEG:(g + 1) * PSEG, :],
                                            x_in[slot][:, g * PSEG:(g + 1) * PSEG, :],
                                            y_out[slot][:, g * PSEG:(g + 1) * PSEG, :],
                                            ALU.subtract).then_inc(rows_out, 1)

                centre(0, 0, 0, 0)
                centre(0, 1, 0, 1)
                for ph in range(NP_):
                    def tiles(i, lo):
                        first, last = lo == 0, lo == NPAIR // BODY - 1
                        for e in range(BODY):
                            p = i * BODY + e
                            if last and e + 2 >= BODY:
                                if ph + 1 < NP_:
                                    centre(ph + 1, e + 2 - BODY, 0, e + 2 - BODY)
                            else:
                                centre(ph, p + 2, i + (e + 2) // BODY, (e + 2) % BODY)
                            if e > 0:
                                add_ratio(ph, p - 1, i, e - 1)
                            elif not first:
                                add_ratio(ph, p - 1, i - 1, BODY - 1)
                            elif ph > 0:
                                add_ratio(ph - 1, NPAIR - 1, TILES // 2 - 1, BODY - 1)
                    looped(pool, NPAIR // BODY, tiles, [0, NPAIR // BODY - 1])
                add_ratio(NP_ - 1, NPAIR - 1, TILES // 2 - 1, BODY - 1)

            @block.scalar
            def _(act):
                act.preload_act_table_set(LN_TABLES)
                act.wait_ge(constants_ready, 1)

                def finish_logs(ph):
                    n = ph + 1
                    act.wait_ge(log_asked, n)
                    nc.scalar.activation(stat_tmp[:, 3, :], stat_tmp[:, 2, :], ACT.Ln, bias=bias_var[:],
                                         scale=VAR_SCALE).then_inc(log_given, 1)
                    act.wait_ge(log_given, 2 * n - 1)
                    nc.scalar.activation(stat_tmp[:, 4, :], stat_tmp[:, 3, :], ACT.Exp, bias=bias_rstd[:],
                                         scale=-0.5).then_inc(log_given, 1)

                def squares(ph, p, par, half):
                    if half == 0:
                        act.wait_ge(rows_centred, ph * NPAIR + p + 1)
                        if not is_opening(ph, p, 2):
                            act.wait_ge(width_done, (ph * NPAIR + p - 1) * UNITS)
                    h = slice(half * 2, half * 2 + 2)
                    nc.scalar.activation(square[par][:, h, :], centred[par][:, h, :], ACT.Square
                                         ).then_inc(rows_squared, 1)

                def take(ph, p, par, k, is_t):
                    u = 2 * k + is_t
                    if u == 0:
                        if isinstance(p, int) and p == 0:
                            act.wait_ge(params_ready, ph + 1)
                        if not is_opening(ph, p, 2):
                            act.wait_ge(num_done, (ph * NPAIR + p - 1) * PSEG)
                    act.wait_ge(width_done, (ph * NPAIR + p) * UNITS + u + 1)
                    src = width_ps[u % 3][:]
                    if is_t:
                        nc.scalar.activation(tT[par][:, k, :], src, ACT.Copy, scale=rvar_col[ph][:, k:k + 1]
                                             ).then_inc(width_taken, 1)
                    else:
                        nc.scalar.activation(sT[par][:, k, :], src, ACT.Square, scale=rstd_col[ph][:, k:k + 1]
                                             ).then_inc(width_taken, 1)

                def invert(ph, p, par, i):
                    base = ph * NPAIR
                    if i == 0 and not is_opening(ph, p, 2):
                        act.wait_ge(ratio_done, base + p - 1)
                    act.wait_ge(den_done, (base + p) * PSEG + i + 1)
                    nc.scalar.activation(recip[par][:, i, :], den_ps[i % 3][:, 0:C], ACT.Ln, bias=bias_ln[:],
                                         scale=LN_SCALE).then_inc(log_done, 1)
                    act.wait_ge(log_done, (base + p) * PSEG + i + 1)
                    nc.scalar.activation(recip[par][:, i, :], recip[par][:, i, :], ACT.Exp, bias=bias_exp[:],
                                         scale=-1.0).then_inc(recip_done, 1)

                def step(ph, p, par):
                    (ph1, p1), (ph2, p2) = in_phase(ph, p + 1), in_phase(ph, p + 2)
                    for what in ("S0", "L0", "T0", "L1", "S1", "Q0", "T1", "L2", "Q1", "S2", "T2", "L3"):
                        n = int(what[1])
                        if what[0] == "L":
                            invert(ph, p, par, n)
                        elif what[0] == "Q":
                            if ph2 < NP_:
                                squares(ph2, p2, par, n)
                        elif ph1 < NP_:
                            take(ph1, p1, 1 - par, n, int(what[0] == "T"))

                finish_logs(0)
                for p in range(2):
                    for half in range(2):
                        squares(0, p, p, half)
                for k in range(KB):
                    take(0, 0, 0, k, 0)
                    take(0, 0, 0, k, 1)
                for ph in range(NP_):
                    def pairs(i, lo):
                        step(ph, i * 2, 0)
                        step(ph, i * 2 + 1, 1)
                    looped(act, NPAIR // 2, pairs, [0, NPAIR // 2 - 1],
                           [(finish_pair(ph) // 2, lambda: finish_logs(ph + 1))] if ph + 1 < NP_ else [])

            @block.tensor
            def _(pe):
                pe.wait_ge(bands_ready, 1)
                pe.wait_ge(constants_ready, 1)

                def finish_sums(ph):
                    n = 3 * ph
                    pe.wait_ge(means_asked, n + 1)
                    for half in range(2):
                        last = nc.tensor.matmul(num_ps[0][:, 0:GROUPS], over_p[:], stat_two[:, 0, half, :],
                                                start=(half == 0), stop=(half == 1))
                    last.then_inc(means_given, 1)
                    pe.wait_ge(means_asked, n + 2)
                    for half in range(2):
                        last = nc.tensor.matmul(num_ps[1][:, 0:GROUPS], over_p[:], stat_two[:, 2, half, :],
                                                start=(half == 0), stop=(half == 1))
                    last.then_inc(means_given, 1)
                    pe.wait_ge(means_asked, n + 3)
                    for k in range(KB):
                        last = nc.tensor.transpose(den_ps[0][:, P * k:P * (k + 1)], rstd_row[:, P * k:P * (k + 1)],
                                                   identity[:])
                    last.then_inc(means_given, 1)
                    pe.wait_ge(params_ready, ph + 1)

                def width_unit(ph, p, par, k, is_t):
                    u = 2 * k + is_t
                    if u == 0:
                        pe.wait_ge(rows_centred, ph * NPAIR + p + 1)
                    if u == 1:
                        pe.wait_ge(rows_squared, (ph * NPAIR + p + 1) * 2)
                    if not (is_opening(ph, p, 1) and u < 3):
                        pe.wait_ge(width_taken, (ph * NPAIR + p) * UNITS + u - 2)
                    data = square[par] if is_t else centred[par]
                    band = band_wc if is_t else band_w
                    bank = width_ps[u % 3]
                    for r in range(2):
                        for j in range(HALVES):
                            at = r * W + HALF_COL[j]
                            last = nc.tensor.matmul(bank[:, at:at + WN], data[:, r * 2 + j, P * k:P * (k + 1)],
                                                    band[:, j, :], start=(r == 0 and j == 0),
                                                    stop=(r == 1 and j == 1), skip_group_check=True)
                    last.then_inc(width_done, 1)

                def channel_unit(ph, p, par, i, is_num):
                    seg = (ph * NPAIR + p) * PSEG + i
                    if i == 0 and not is_num:
                        pe.wait_ge(width_taken, (ph * NPAIR + p + 1) * UNITS)
                    if is_num:
                        bank, data = num_ps[i % 2], sT[par]
                        if not (is_opening(ph, p, 1) and i < 2):
                            pe.wait_ge(num_used, seg - 1)
                    else:
                        bank, data = den_ps[i % 3], tT[par]
                        if not (is_opening(ph, p, 1) and i < 3):
                            pe.wait_ge(den_used, seg if i == 0 else seg - 2 if i == 3 else seg - 3)
                    at = (i // 2) * W + (i % 2) * P
                    for k in range(KB):
                        lo, hi = c_span[k]
                        last = nc.tensor.matmul(bank[:, lo:hi], data[:, k, at:at + P], band_c[k][:],
                                                start=(k == 0), stop=(k == KB - 1), skip_group_check=True)
                    last.then_inc(num_done if is_num else den_done, 1)

                def step(ph, p, par):
                    ph1, p1 = in_phase(ph, p + 1)
                    for what in ("S0", "D0", "T0", "D1", "S1", "N0", "T1", "D2", "S2", "N1", "T2", "D3", "N2", "N3"):
                        n = int(what[1])
                        if what[0] in "DN":
                            channel_unit(ph, p, par, n, what[0] == "N")
                        elif ph1 < NP_:
                            width_unit(ph1, p1, 1 - par, n, int(what[0] == "T"))

                finish_sums(0)
                for k in range(KB):
                    width_unit(0, 0, 0, k, 0)
                    width_unit(0, 0, 0, k, 1)
                for ph in range(NP_):
                    def pairs(i, lo):
                        step(ph, i * 2, 0)
                        step(ph, i * 2 + 1, 1)
                    looped(pe, NPAIR // 2, pairs, [0, NPAIR // 2 - 1],
                           [(finish_pair(ph) // 2, lambda: finish_sums(ph + 1))] if ph + 1 < NP_ else [])

            @block.vector
            def _(dve):
                links = [0]

                def link(instruction):
                    links[0] += 1
                    instruction.then_inc(dve_chain, 1)
                    dve.wait_ge(dve_chain, links[0])

                for j in range(HALVES):
                    nc.vector.memset(band_w[:, j, :], 1.0)
                    nc.vector.memset(band_wc[:, j, :], float(W_BOX))
                for k in range(KB):
                    nc.vector.memset(band_c[k][:], 1.0)
                nc.vector.memset(identity[:], 1.0).then_inc(ones_set, 1)
                nc.vector.memset(over_p[:], 0.5 / P)
                nc.vector.memset(bias_ln[:], TINY * LN_SCALE)
                nc.vector.memset(bias_exp[:], LN2 * 38)
                nc.vector.memset(bias_var[:], EPS * VAR_SCALE)
                nc.vector.memset(bias_rstd[:], -LN2 * 20).then_inc(constants_ready, 1)

                def measure(tile, groups, stats, column):
                    for g in groups:
                        last = nc.vector.bn_stats(stats[:, g, bass.ds(column * 6, 6)],
                                                  tile[:, :, CG * g:CG * (g + 1)])
                    return last

                def lane_totals(b, half, groups, stats):
                    for g in groups:
                        last = nc.vector.bn_aggr(lane_mv[b][:, half, g, :], stats[:, g, :])
                    link(last)

                for half in range(2):
                    with dve.Fori(0, SPLIT // 4) as i:
                        for s in range(4):
                            dve.wait_ge(in_landed[s], (half * (SPLIT // 4) + i + 1) * 16)
                            measure(stat_tiles[s], range(GROUPS), out_stats, i * 4 + s).then_inc(tile_measured, 1)
                    dve.wait_ge(tile_measured, (half + 1) * SPLIT)
                    lane_totals(0, half, range(GROUPS), out_stats)
                for s in range(UPFRONT):
                    dve.wait_ge(in_landed[s], (TILES // 4 + 1) * 16)
                    measure(stat_tiles[s], range(GROUPS), beside_stats, s).then_inc(tile_measured, 1)

                dve.wait_ge(bands_cut, 2 * HALVES + KB + 1)
                for d in range(REACH):
                    for j, col in ((0, d), (1, WN - 1 - d)):
                        last = nc.vector.tensor_scalar(band_wc[:, j, col:col + 1], band_w[:, j, col:col + 1],
                                                       float(REACH + 1 + d), None, ALU.mult)
                last.then_inc(bands_ready, 1)

                def finish(ph):
                    b = PHASES[ph][1]
                    asked, logs = 3 * ph, ph + 1
                    mean_l, var_l = lane_mv[b][:, :, :, 0], lane_mv[b][:, :, :, 1]
                    nc.vector.tensor_copy(stat_two[:, 0, :, :], mean_l).then_inc(means_asked, 1)
                    dve.wait_ge(means_given, asked + 1)
                    mean = num_ps[0][:, 0:GROUPS]
                    link(nc.vector.tensor_tensor(stat_two[:, 1, :, :], mean_l,
                                                 mean.unsqueeze(1).to_broadcast([P, 2, GROUPS]), ALU.subtract))
                    link(nc.vector.tensor_tensor(stat_two[:, 1, :, :], stat_two[:, 1, :, :], stat_two[:, 1, :, :],
                                                 ALU.mult))
                    nc.vector.tensor_tensor(stat_two[:, 2, :, :], stat_two[:, 1, :, :], var_l, ALU.add
                                            ).then_inc(means_asked, 1)
                    nc.vector.tensor_copy(mean_row[ph % 2][:].rearrange("p (g c) -> p g c", c=CG),
                                          mean.unsqueeze(2).to_broadcast([P, GROUPS, CG]))
                    dve.wait_ge(means_given, asked + 2)
                    nc.vector.tensor_copy(stat_tmp[:, 2, :], num_ps[1][:, 0:GROUPS]).then_inc(log_asked, 1)
                    dve.wait_ge(log_asked, logs)
                    link(nc.vector.tensor_scalar(stat_tmp[:, 0, :], stat_tmp[:, 2, :], EPS, None, ALU.add))
                    dve.wait_ge(log_given, 2 * logs)
                    link(nc.vector.tensor_tensor(stat_tmp[:, 1, :], stat_tmp[:, 4, :], stat_tmp[:, 4, :], ALU.mult))
                    link(nc.vector.tensor_tensor(stat_tmp[:, 1, :], stat_tmp[:, 1, :], stat_tmp[:, 0, :], ALU.mult))
                    link(nc.vector.tensor_scalar(stat_tmp[:, 1, :], stat_tmp[:, 1, :], -0.5, 1.5, ALU.mult, ALU.add))
                    link(nc.vector.tensor_tensor(stat_tmp[:, 1, :], stat_tmp[:, 1, :], stat_tmp[:, 4, :], ALU.mult))
                    nc.vector.tensor_copy(rstd_row[:].rearrange("p (g c) -> p g c", c=CG),
                                          stat_tmp[:, 1, :].unsqueeze(2).to_broadcast([P, GROUPS, CG])
                                          ).then_inc(means_asked, 1)
                    dve.wait_ge(means_given, asked + 3)
                    link(nc.vector.tensor_copy(rstd_col[ph][:], den_ps[0][:, 0:C].rearrange(
                        "p (k n) -> p k n", n=P)[:, :, 0]))
                    nc.vector.tensor_tensor(rvar_col[ph][:], rstd_col[ph][:], rstd_col[ph][:], ALU.mult
                                            ).then_inc(params_ready, 1)
                    dve.wait_ge(params_ready, ph + 1)

                def approach(ph, p, par, i):
                    dve.wait_ge(recip_done, (ph * NPAIR + p) * PSEG + i + 1)
                    if i == 0 and not is_opening(ph, p, 1):
                        dve.wait_ge(ratio_done, ph * NPAIR + p)
                    nc.vector.scalar_tensor_tensor(newton[:, i, :], den_ps[i % 3][:, 0:C], TINY,
                                                   recip[par][:, i, :], ALU.add, ALU.mult).then_inc(den_used, 1)

                def weigh(ph, p, par, i):
                    dve.wait_ge(num_done, (ph * NPAIR + p) * PSEG + i + 1)
                    nc.vector.scalar_tensor_tensor(recip[par][:, i, :], num_ps[i % 2][:, 0:C], TINY,
                                                   recip[par][:, i, :], ALU.add, ALU.mult).then_inc(num_used, 1)

                def divide(ph, i, p, e):
                    slot, g = e // PAIRS, e % PAIRS
                    dve.wait_ge(num_used, (ph * NPAIR + p + 1) * PSEG)
                    dve.wait_ge(den_used, (ph * NPAIR + p + 1) * PSEG)
                    if g == 0 and not is_opening(ph, p, BODY):
                        dve.wait_ge(out_landed[slot], (ph * (TILES // 2) + i) * 16)
                    nc.vector.scalar_tensor_tensor(y_out[slot][:, g * PSEG:(g + 1) * PSEG, :], newton[:], 2.0,
                                                   recip[e % 2][:], ALU.subtract, ALU.mult).then_inc(ratio_done, 1)

                def measure_output(ph, i, lo, e):
                    q, early = e % PAIRS, e < PAIRS
                    quarter = range(q * chunk, (q + 1) * chunk)
                    layer, b = PHASES[ph]
                    if lo == 0 and early:
                        if not 0 < ph <= B:
                            return
                        tile, column, ends = ph * TILES - 1, TILES - SPLIT - 1, (PHASES[ph - 1][1], 1)
                    elif layer > 0:
                        return
                    else:
                        m = i * 2 + (-1 if early else 0)
                        tile = ph * TILES + m
                        column = m - SPLIT if lo > MID or (lo == MID and not early) else m
                        ends = (b, 0) if lo == MID and early else None
                    if q == 0:
                        dve.wait_ge(rows_out, (tile + 1) * PAIRS)
                    measure(y_out[1 if early else 0], quarter, out_stats, column).then_inc(stats_done, 1)
                    if ends:
                        dve.wait_ge(stats_done, tile * PAIRS + q + 1)
                        lane_totals(*ends, quarter, out_stats)

                def measure_beside(ph, i, lo, e):
                    q = e % PAIRS
                    if ph > 0 or lo >= BESIDE_END or q == 3:
                        return
                    third = range(GROUPS * q // 3, GROUPS * (q + 1) // 3)
                    n = i * 2 + e // PAIRS
                    if lo == BESIDE_SPLIT and e < PAIRS:
                        if q == 0:
                            dve.wait_ge(beside_done, n)
                        lane_totals(1, 0, third, beside_stats)
                    if q == 0:
                        dve.wait_ge(beside_landed, (n + 1) * 16)
                    column = n + UPFRONT - (SPLIT if lo >= BESIDE_SPLIT else 0)
                    last = measure(beside, third, beside_stats, column)
                    if q == 2:
                        last.then_inc(beside_done, 1)

                def finish_next(ph):
                    if ph == 0:
                        dve.wait_ge(beside_done, BESIDE)
                        lane_totals(1, 1, range(GROUPS), beside_stats)
                    finish(ph + 1)

                finish(0)
                for ph in range(NP_):
                    def tiles(i, lo):
                        for e in range(BODY):
                            p, par = i * BODY + e, e % 2
                            approach(ph, p, par, 0)
                            approach(ph, p, par, 1)
                            weigh(ph, p, par, 0)
                            measure_beside(ph, i, lo, e)
                            approach(ph, p, par, 2)
                            weigh(ph, p, par, 1)
                            approach(ph, p, par, 3)
                            weigh(ph, p, par, 2)
                            weigh(ph, p, par, 3)
                            divide(ph, i, p, e)
                            measure_output(ph, i, lo, e)
                    peeled = [0] + [MID] * (PHASES[ph][0] == 0) + [BESIDE_SPLIT] * (ph == 0)
                    looped(dve, NPAIR // BODY, tiles, peeled,
                           [(finish_pair(ph) // BODY, lambda: finish_next(ph))] if ph + 1 < NP_ else [])


def kernel(x):
    import numpy as np
    import concourse.bacc as bacc
    from concourse.bass_utils import run_bass_kernel_spmd

    nc = bacc.Bacc("TRN2", target_bir_lowering=False, num_devices=1, dynamic_dma_scratch_size=1024)
    a = np.ascontiguousarray(x)
    xin = nc.dram_tensor("in_x_dram", a.shape, mybir.dt.from_np(a.dtype), kind="ExternalInput").ap()
    out = nc.dram_tensor("out_0_dram", a.shape, mybir.dt.from_np(a.dtype), kind="ExternalOutput").ap()
    similarity_layers_kernel(nc, xin, out)
    r = run_bass_kernel_spmd(nc, [{"in_x_dram": a}], core_ids=[0])
    return r.results[0]["out_0_dram"]
```

```python
from contextlib import ExitStack

import concourse.bass as bass
from concourse import mybir
from concourse.alu_op_type import AluOpType as ALU

F32 = mybir.dt.float32
ACT = mybir.ActivationFunctionType

P = 128
GROUPS = 32
EPS = 1e-5
W_BOX = 5
C_BOX = 20
C_LO = C_BOX // 2
C_HI = C_BOX - C_LO - 1
TILE_ROWS = 8
PAIRS = TILE_ROWS // 2
BODY = 2 * PAIRS
TINY = 2.0 ** -100
LN_SCALE = 2.0 ** 38
VAR_SCALE = 2.0 ** -40
LN2 = 0.6931471805599453
LN_TABLES = "natural_log_exp_and_others"


def similarity_layers_kernel(nc, x, out):
    B, H, W, C = x.shape
    HALVES = W // P
    KB = C // P
    CG = C // GROUPS
    SEGS = TILE_ROWS * HALVES
    PSEG = 2 * HALVES
    UNITS = 2 * KB
    TILES = H // TILE_ROWS
    NPAIR = H // 2
    LAYERS = 2
    PHASES = [(layer, b) for layer in range(LAYERS) for b in range(B)]
    NP_ = len(PHASES)
    assert W == 2 * P and C == 3 * P and TILES % 4 == 0 and B == 2 and TILES >= 8
    SPLIT = TILES // 2
    MID = SPLIT // 2
    UPFRONT = 2
    BESIDE = TILES - UPFRONT
    BESIDE_SPLIT = (SPLIT - UPFRONT) // 2
    BESIDE_END = BESIDE // 2
    REACH = W_BOX // 2
    WN = P + REACH
    HALF_COL = [0, P - REACH]
    c_span = [(max(0, P * k - C_HI), min(C, P * (k + 1) + C_LO)) for k in range(KB)]

    def tiles_of(t, b):
        return t[b].rearrange("h (j p) c -> p (h j) c", p=P)

    x1 = nc.dram_tensor("first_layer_out", x.shape, F32, kind="Internal").ap()
    source = [x, x1]
    target = [x1, out]

    with ExitStack() as ctx:
        def sb(name, shape, dt=F32):
            return ctx.enter_context(nc.sbuf_tensor(name, shape, dt))

        def sem(name):
            return ctx.enter_context(nc.semaphore(name))

        x_in = [sb(f"x_in{i}", [P, SEGS, C]) for i in range(2)]
        y_out = [sb(f"y_out{i}", [P, SEGS, C]) for i in range(2)]
        stat_tiles = [x_in[0], x_in[1], y_out[0], y_out[1]]
        centred = [sb(f"centred{i}", [P, PSEG, C]) for i in range(2)]
        square = [sb(f"square{i}", [P, PSEG, C]) for i in range(2)]
        sT = [sb(f"sT{i}", [P, KB, 2 * W]) for i in range(2)]
        tT = [sb(f"tT{i}", [P, KB, 2 * W]) for i in range(2)]
        recip = [sb(f"recip{i}", [P, PSEG, C]) for i in range(2)]
        newton = sb("newton", [P, PSEG, C])
        beside = sb("beside", [P, SEGS, C])
        out_stats = sb("out_stats", [P, GROUPS, SPLIT * 6])
        beside_stats = sb("beside_stats", [P, GROUPS, SPLIT * 6])
        lane_mv = [sb(f"lane_mv{b}", [P, 2, GROUPS, 2]) for b in range(B)]
        stat_tmp = sb("stat_tmp", [P, 5, GROUPS])
        stat_two = sb("stat_two", [P, 3, 2, GROUPS])
        rstd_row = sb("rstd_row", [P, C])
        mean_row = [sb(f"mean_row{i}", [P, C]) for i in range(2)]
        rstd_col = [sb(f"rstd_col{i}", [P, KB]) for i in range(NP_)]
        rvar_col = [sb(f"rvar_col{i}", [P, KB]) for i in range(NP_)]
        band_w = sb("band_w", [P, HALVES, WN])
        band_wc = sb("band_wc", [P, HALVES, WN])
        band_c = [sb(f"band_c{k}", [P, c_span[k][1] - c_span[k][0]]) for k in range(KB)]
        identity = sb("identity", [P, P])
        over_p = sb("over_p", [P, P])
        bias_ln = sb("bias_ln", [P, 1])
        bias_exp = sb("bias_exp", [P, 1])
        bias_var = sb("bias_var", [P, 1])
        bias_rstd = sb("bias_rstd", [P, 1])

        width_ps = [ctx.enter_context(nc.psum_tensor(f"width_ps{i}", [P, 2 * W], F32)) for i in range(3)]
        den_ps = [ctx.enter_context(nc.psum_tensor(f"den_ps{i}", [P, 512], F32)) for i in range(3)]
        num_ps = [ctx.enter_context(nc.psum_tensor(f"num_ps{i}", [P, 512], F32)) for i in range(2)]

        in_landed = [sem(f"in_landed{i}") for i in range(4)]
        out_landed = [sem(f"out_landed{i}") for i in range(2)]
        ones_set = sem("ones_set")
        bands_cut = sem("bands_cut")
        bands_ready = sem("bands_ready")
        constants_ready = sem("constants_ready")
        pool_chain = sem("pool_chain")
        beside_landed = sem("beside_landed")
        beside_done = sem("beside_done")
        tile_measured = sem("tile_measured")
        rows_centred = sem("rows_centred")
        rows_squared = sem("rows_squared")
        width_done = sem("width_done")
        width_taken = sem("width_taken")
        den_done = sem("den_done")
        num_done = sem("num_done")
        log_done = sem("log_done")
        recip_done = sem("recip_done")
        den_used = sem("den_used")
        num_used = sem("num_used")
        ratio_done = sem("ratio_done")
        rows_out = sem("rows_out")
        stats_done = sem("stats_done")
        dve_chain = sem("dve_chain")
        means_asked = sem("means_asked")
        means_given = sem("means_given")
        log_asked = sem("log_asked")
        log_given = sem("log_given")
        mean_ready = sem("mean_ready")
        params_ready = sem("params_ready")

        def pairs_before(ph):
            return ph * NPAIR

        def in_phase(ph, p):
            return (ph + 1, p - NPAIR) if isinstance(p, int) and p >= NPAIR else (ph, p)

        def is_opening(ph, p, n):
            return ph == 0 and isinstance(p, int) and p < n

        def looped(eng, n, body, peeled, cuts=()):
            calls = {at: call for at, call in cuts}
            starts = sorted({0, n} | set(calls) | {p for p in peeled} | {p + 1 for p in peeled if p + 1 < n})
            for lo, hi in zip(starts, starts[1:]):
                if calls.get(lo) is not None:
                    calls[lo]()
                if lo in peeled:
                    body(lo, lo)
                elif hi > lo:
                    with eng.Fori(lo, hi) as i:
                        body(i, lo)

        def finish_pair(ph):
            return BESIDE_END * BODY if ph == 0 else BODY

        chunk = GROUPS // PAIRS

        with nc.Block() as block:

            @block.sync
            def _(sp):
                view = tiles_of(x, 0)

                def measure_loads(i, lo):
                    for s in range(4):
                        if lo > 0:
                            sp.wait_ge(tile_measured, i * 4 + s - 3)
                        sp.dma_start(stat_tiles[s][:], view[:, bass.ds((i * 4 + s) * SEGS, SEGS), :]
                                     ).then_inc(in_landed[s], 16)
                looped(sp, TILES // 4, measure_loads, [0])
                for s in range(2):
                    sp.wait_ge(tile_measured, TILES - 3 + s)
                    sp.dma_start(x_in[s][:], tiles_of(x, 0)[:, s * SEGS:(s + 1) * SEGS, :]
                                 ).then_inc(in_landed[s], 16)
                def load_beside(n):
                    sp.dma_start(beside[:], tiles_of(x, 1)[:, bass.ds((UPFRONT + n) * SEGS, SEGS), :]
                                 ).then_inc(beside_landed, 16)
                for s in range(UPFRONT):
                    sp.wait_ge(tile_measured, TILES - 1 + s)
                    sp.dma_start(y_out[s][:], tiles_of(x, 1)[:, s * SEGS:(s + 1) * SEGS, :]
                                 ).then_inc(in_landed[2 + s], 16)
                    if s == 0:
                        load_beside(0)
                sp.wait_ge(beside_done, 3)
                load_beside(1)
                for ph, (layer, b) in enumerate(PHASES):
                    src = tiles_of(source[layer], b)
                    dst = tiles_of(target[layer], b)
                    bodies = TILES // 2

                    def move_tiles(i, lo):
                        last = lo == bodies - 1
                        for s in range(2):
                            m = i * 2 + s
                            if last and s == 1 and ph == NP_ - 1:
                                for g in range(PAIRS):
                                    sp.wait_ge(rows_out, pairs_before(ph) + m * PAIRS + g + 1)
                                    sp.dma_start(dst[:, m * SEGS + g * PSEG:m * SEGS + (g + 1) * PSEG, :],
                                                 y_out[1][:, g * PSEG:(g + 1) * PSEG, :]
                                                 ).then_inc(out_landed[1], 16)
                                continue
                            sp.wait_ge(rows_out, pairs_before(ph) + (m + 1) * PAIRS)
                            if not last:
                                sp.dma_start(x_in[s][:], src[:, bass.ds((m + 2) * SEGS, SEGS), :]
                                             ).then_inc(in_landed[s], 16)
                            elif ph + 1 < NP_:
                                nl, nb = PHASES[ph + 1]
                                if nl > 0:
                                    for o in range(2):
                                        sp.wait_ge(out_landed[o], 16 * (TILES // 2) * (nb + 1))
                                sp.dma_start(x_in[s][:], tiles_of(source[nl], nb)[:, s * SEGS:(s + 1) * SEGS, :]
                                             ).then_inc(in_landed[s], 16)
                            sp.dma_start(dst[:, bass.ds(m * SEGS, SEGS), :], y_out[s][:]
                                         ).then_inc(out_landed[s], 16)
                            if ph == 0 and lo < BESIDE_END - 1:
                                sp.wait_ge(beside_done, (m + 2) * 3)
                                load_beside(m + 2)
                    looped(sp, bodies, move_tiles, [bodies - 1], [(BESIDE_END - 1, None)] if ph == 0 else [])
                for s in range(2):
                    sp.wait_ge(out_landed[s], 16 * ((TILES // 2) * NP_ + s * (PAIRS - 1)))

            def loads_before(ph):
                return TILES // 4 + ph * (TILES // 2)

            @block.gpsimd
            def _(pool):
                pool.wait_ge(ones_set, 1)
                cuts = 0
                for j in range(HALVES):
                    for band in (band_w, band_wc):
                        off = HALF_COL[j] - P * j
                        nc.gpsimd.affine_select(out=band[:, j, :], in_=band[:, j, :], compare_op=ALU.is_ge, fill=0.0,
                                                base=off + REACH, pattern=[[1, WN]], channel_multiplier=-1
                                                ).then_inc(pool_chain, 1)
                        cuts += 1
                        pool.wait_ge(pool_chain, cuts)
                        nc.gpsimd.affine_select(out=band[:, j, :], in_=band[:, j, :], compare_op=ALU.is_ge, fill=0.0,
                                                base=REACH - off, pattern=[[-1, WN]], channel_multiplier=1
                                                ).then_inc(bands_cut, 1)
                for k in range(KB):
                    lo, hi = c_span[k]
                    n = hi - lo
                    nc.gpsimd.affine_select(out=band_c[k][:], in_=band_c[k][:], compare_op=ALU.is_ge, fill=0.0,
                                            base=lo - P * k + C_HI, pattern=[[1, n]], channel_multiplier=-1
                                            ).then_inc(pool_chain, 1)
                    cuts += 1
                    pool.wait_ge(pool_chain, cuts)
                    nc.gpsimd.affine_select(out=band_c[k][:], in_=band_c[k][:], compare_op=ALU.is_ge, fill=0.0,
                                            base=P * k + C_LO - lo, pattern=[[-1, n]], channel_multiplier=1
                                            ).then_inc(bands_cut, 1)
                nc.gpsimd.affine_select(out=identity[:], in_=identity[:], compare_op=ALU.is_equal, fill=0.0, base=0,
                                        pattern=[[1, P]], channel_multiplier=-1).then_inc(bands_cut, 1)

                def centre(ph, p, i, e):
                    slot, g = e // PAIRS, e % PAIRS
                    if isinstance(p, int) and p == 0:
                        pool.wait_ge(mean_ready, ph + 1)
                    if g == 0:
                        pool.wait_ge(in_landed[slot], (loads_before(ph) + i + 1) * 16)
                    if not (ph == 0 and isinstance(p, int) and p < 2):
                        pool.wait_ge(width_done, (ph * NPAIR + p - 1) * UNITS)
                    nc.gpsimd.tensor_tensor(centred[e % 2][:], x_in[slot][:, g * PSEG:(g + 1) * PSEG, :],
                                            mean_row[ph % 2][:].unsqueeze(1).to_broadcast([P, PSEG, C]),
                                            ALU.subtract).then_inc(rows_centred, 1)

                def add_ratio(ph, p, i, e):
                    slot, g = e // PAIRS, e % PAIRS
                    pool.wait_ge(ratio_done, ph * NPAIR + p + 1)
                    nc.gpsimd.tensor_tensor(y_out[slot][:, g * PSEG:(g + 1) * PSEG, :],
                                            x_in[slot][:, g * PSEG:(g + 1) * PSEG, :],
                                            y_out[slot][:, g * PSEG:(g + 1) * PSEG, :],
                                            ALU.subtract).then_inc(rows_out, 1)

                centre(0, 0, 0, 0)
                centre(0, 1, 0, 1)
                for ph in range(NP_):
                    def tiles(i, lo):
                        first, last = lo == 0, lo == NPAIR // BODY - 1
                        for e in range(BODY):
                            p = i * BODY + e
                            if last and e + 2 >= BODY:
                                if ph + 1 < NP_:
                                    centre(ph + 1, e + 2 - BODY, 0, e + 2 - BODY)
                            else:
                                centre(ph, p + 2, i + (e + 2) // BODY, (e + 2) % BODY)
                            if e > 0:
                                add_ratio(ph, p - 1, i, e - 1)
                            elif not first:
                                add_ratio(ph, p - 1, i - 1, BODY - 1)
                            elif ph > 0:
                                add_ratio(ph - 1, NPAIR - 1, TILES // 2 - 1, BODY - 1)
                    looped(pool, NPAIR // BODY, tiles, [0, NPAIR // BODY - 1])
                add_ratio(NP_ - 1, NPAIR - 1, TILES // 2 - 1, BODY - 1)

            @block.scalar
            def _(act):
                act.preload_act_table_set(LN_TABLES)
                act.wait_ge(constants_ready, 1)

                def finish_logs(ph):
                    n = ph + 1
                    act.wait_ge(log_asked, n)
                    nc.scalar.activation(stat_tmp[:, 3, :], stat_tmp[:, 2, :], ACT.Ln, bias=bias_var[:],
                                         scale=VAR_SCALE).then_inc(log_given, 1)
                    act.wait_ge(log_given, 2 * n - 1)
                    nc.scalar.activation(stat_tmp[:, 4, :], stat_tmp[:, 3, :], ACT.Exp, bias=bias_rstd[:],
                                         scale=-0.5).then_inc(log_given, 1)

                def squares(ph, p, par, half):
                    if half == 0:
                        act.wait_ge(rows_centred, ph * NPAIR + p + 1)
                        if not is_opening(ph, p, 2):
                            act.wait_ge(width_done, (ph * NPAIR + p - 1) * UNITS)
                    h = slice(half * 2, half * 2 + 2)
                    nc.scalar.activation(square[par][:, h, :], centred[par][:, h, :], ACT.Square
                                         ).then_inc(rows_squared, 1)

                def take(ph, p, par, k, is_t):
                    u = 2 * k + is_t
                    if u == 0:
                        if isinstance(p, int) and p == 0:
                            act.wait_ge(params_ready, ph + 1)
                        if not is_opening(ph, p, 2):
                            act.wait_ge(num_done, (ph * NPAIR + p - 1) * PSEG)
                    act.wait_ge(width_done, (ph * NPAIR + p) * UNITS + u + 1)
                    src = width_ps[u % 3][:]
                    if is_t:
                        nc.scalar.activation(tT[par][:, k, :], src, ACT.Copy, scale=rvar_col[ph][:, k:k + 1]
                                             ).then_inc(width_taken, 1)
                    else:
                        nc.scalar.activation(sT[par][:, k, :], src, ACT.Square, scale=rstd_col[ph][:, k:k + 1]
                                             ).then_inc(width_taken, 1)

                def invert(ph, p, par, i):
                    base = ph * NPAIR
                    if i == 0 and not is_opening(ph, p, 2):
                        act.wait_ge(ratio_done, base + p - 1)
                    act.wait_ge(den_done, (base + p) * PSEG + i + 1)
                    nc.scalar.activation(recip[par][:, i, :], den_ps[i % 3][:, 0:C], ACT.Ln, bias=bias_ln[:],
                                         scale=LN_SCALE).then_inc(log_done, 1)
                    act.wait_ge(log_done, (base + p) * PSEG + i + 1)
                    nc.scalar.activation(recip[par][:, i, :], recip[par][:, i, :], ACT.Exp, bias=bias_exp[:],
                                         scale=-1.0).then_inc(recip_done, 1)

                def step(ph, p, par):
                    (ph1, p1), (ph2, p2) = in_phase(ph, p + 1), in_phase(ph, p + 2)
                    for what in ("S0", "L0", "T0", "L1", "S1", "Q0", "T1", "L2", "Q1", "S2", "T2", "L3"):
                        n = int(what[1])
                        if what[0] == "L":
                            invert(ph, p, par, n)
                        elif what[0] == "Q":
                            if ph2 < NP_:
                                squares(ph2, p2, par, n)
                        elif ph1 < NP_:
                            take(ph1, p1, 1 - par, n, int(what[0] == "T"))

                finish_logs(0)
                for p in range(2):
                    for half in range(2):
                        squares(0, p, p, half)
                for k in range(KB):
                    take(0, 0, 0, k, 0)
                    take(0, 0, 0, k, 1)
                for ph in range(NP_):
                    def pairs(i, lo):
                        step(ph, i * 2, 0)
                        step(ph, i * 2 + 1, 1)
                    looped(act, NPAIR // 2, pairs, [0, NPAIR // 2 - 1],
                           [(finish_pair(ph) // 2, lambda: finish_logs(ph + 1))] if ph + 1 < NP_ else [])

            @block.tensor
            def _(pe):
                pe.wait_ge(bands_ready, 1)
                pe.wait_ge(constants_ready, 1)

                def finish_part(ph, part):
                    pe.wait_ge(means_asked, 3 * ph + part)
                    if part < 3:
                        for half in range(2):
                            last = nc.tensor.matmul(num_ps[part - 1][:, 0:GROUPS], over_p[:],
                                                    stat_two[:, 2 * (part - 1), half, :],
                                                    start=(half == 0), stop=(half == 1))
                    else:
                        for k in range(KB):
                            last = nc.tensor.transpose(den_ps[2][:, P * k:P * (k + 1)],
                                                       rstd_row[:, P * k:P * (k + 1)], identity[:])
                    last.then_inc(means_given, 1)

                def width_unit(ph, p, par, k, is_t):
                    u = 2 * k + is_t
                    if u == 0:
                        pe.wait_ge(rows_centred, ph * NPAIR + p + 1)
                    if u == 1:
                        pe.wait_ge(rows_squared, (ph * NPAIR + p + 1) * 2)
                    if not (is_opening(ph, p, 1) and u < 3):
                        pe.wait_ge(width_taken, (ph * NPAIR + p) * UNITS + u - 2)
                    data = square[par] if is_t else centred[par]
                    band = band_wc if is_t else band_w
                    bank = width_ps[u % 3]
                    for r in range(2):
                        for j in range(HALVES):
                            at = r * W + HALF_COL[j]
                            last = nc.tensor.matmul(bank[:, at:at + WN], data[:, r * 2 + j, P * k:P * (k + 1)],
                                                    band[:, j, :], start=(r == 0 and j == 0),
                                                    stop=(r == 1 and j == 1), skip_group_check=True)
                    last.then_inc(width_done, 1)

                def channel_unit(ph, p, par, i, is_num):
                    seg = (ph * NPAIR + p) * PSEG + i
                    if i == 0 and not is_num:
                        pe.wait_ge(width_taken, (ph * NPAIR + p + 1) * UNITS)
                    if is_num:
                        bank, data = num_ps[i % 2], sT[par]
                        if not (is_opening(ph, p, 1) and i < 2):
                            pe.wait_ge(num_used, seg - 1)
                    else:
                        bank, data = den_ps[i % 3], tT[par]
                        if not (is_opening(ph, p, 1) and i < 3):
                            pe.wait_ge(den_used, seg if i == 0 else seg - 2 if i == 3 else seg - 3)
                    at = (i // 2) * W + (i % 2) * P
                    for k in range(KB):
                        lo, hi = c_span[k]
                        last = nc.tensor.matmul(bank[:, lo:hi], data[:, k, at:at + P], band_c[k][:],
                                                start=(k == 0), stop=(k == KB - 1), skip_group_check=True)
                    last.then_inc(num_done if is_num else den_done, 1)

                def step(ph, p, par):
                    ph1, p1 = in_phase(ph, p + 1)
                    finishing = ph + 1 < NP_ and isinstance(p, int) and p == finish_pair(ph)
                    for what in ("S0", "F1", "D0", "F2", "T0", "D1", "S1", "F3", "N0", "T1", "D2", "S2", "N1", "T2",
                                 "D3", "N2", "N3"):
                        n = int(what[1])
                        if what[0] == "F":
                            if finishing:
                                finish_part(ph + 1, n)
                        elif what[0] in "DN":
                            if what == "D2" and finishing:
                                pe.wait_ge(params_ready, ph + 2)
                            channel_unit(ph, p, par, n, what[0] == "N")
                        elif ph1 < NP_:
                            width_unit(ph1, p1, 1 - par, n, int(what[0] == "T"))

                for part in (1, 2, 3):
                    finish_part(0, part)
                pe.wait_ge(params_ready, 1)
                for k in range(KB):
                    width_unit(0, 0, 0, k, 0)
                    width_unit(0, 0, 0, k, 1)
                for ph in range(NP_):
                    def pairs(i, lo):
                        step(ph, i * 2, 0)
                        step(ph, i * 2 + 1, 1)
                    looped(pe, NPAIR // 2, pairs,
                           [0, NPAIR // 2 - 1] + ([finish_pair(ph) // 2] if ph + 1 < NP_ else []))

            @block.vector
            def _(dve):
                links = [0]

                def link(instruction):
                    links[0] += 1
                    instruction.then_inc(dve_chain, 1)
                    dve.wait_ge(dve_chain, links[0])

                for j in range(HALVES):
                    nc.vector.memset(band_w[:, j, :], 1.0)
                    nc.vector.memset(band_wc[:, j, :], float(W_BOX))
                for k in range(KB):
                    nc.vector.memset(band_c[k][:], 1.0)
                nc.vector.memset(identity[:], 1.0).then_inc(ones_set, 1)
                nc.vector.memset(over_p[:], 0.5 / P)
                nc.vector.memset(bias_ln[:], TINY * LN_SCALE)
                nc.vector.memset(bias_exp[:], LN2 * 38)
                nc.vector.memset(bias_var[:], EPS * VAR_SCALE)
                nc.vector.memset(bias_rstd[:], -LN2 * 20).then_inc(constants_ready, 1)

                def measure(tile, groups, stats, column):
                    for g in groups:
                        last = nc.vector.bn_stats(stats[:, g, bass.ds(column * 6, 6)],
                                                  tile[:, :, CG * g:CG * (g + 1)])
                    return last

                def lane_totals(b, half, groups, stats):
                    for g in groups:
                        last = nc.vector.bn_aggr(lane_mv[b][:, half, g, :], stats[:, g, :])
                    link(last)

                for half in range(2):
                    with dve.Fori(0, SPLIT // 4) as i:
                        for s in range(4):
                            dve.wait_ge(in_landed[s], (half * (SPLIT // 4) + i + 1) * 16)
                            measure(stat_tiles[s], range(GROUPS), out_stats, i * 4 + s).then_inc(tile_measured, 1)
                    dve.wait_ge(tile_measured, (half + 1) * SPLIT)
                    lane_totals(0, half, range(GROUPS), out_stats)

                dve.wait_ge(bands_cut, 2 * HALVES + KB + 1)
                for d in range(REACH):
                    for j, col in ((0, d), (1, WN - 1 - d)):
                        last = nc.vector.tensor_scalar(band_wc[:, j, col:col + 1], band_w[:, j, col:col + 1],
                                                       float(REACH + 1 + d), None, ALU.mult)
                last.then_inc(bands_ready, 1)

                def ask_means(ph):
                    nc.vector.tensor_copy(stat_two[:, 0, :, :], lane_mv[PHASES[ph][1]][:, :, :, 0]
                                          ).then_inc(means_asked, 1)

                def finish(ph):
                    b = PHASES[ph][1]
                    asked, logs = 3 * ph, ph + 1
                    mean_l, var_l = lane_mv[b][:, :, :, 0], lane_mv[b][:, :, :, 1]
                    dve.wait_ge(means_given, asked + 1)
                    mean = num_ps[0][:, 0:GROUPS]
                    link(nc.vector.tensor_tensor(stat_two[:, 1, :, :], mean_l,
                                                 mean.unsqueeze(1).to_broadcast([P, 2, GROUPS]), ALU.subtract))
                    link(nc.vector.tensor_tensor(stat_two[:, 1, :, :], stat_two[:, 1, :, :], stat_two[:, 1, :, :],
                                                 ALU.mult))
                    nc.vector.tensor_tensor(stat_two[:, 2, :, :], stat_two[:, 1, :, :], var_l, ALU.add
                                            ).then_inc(means_asked, 1)
                    nc.vector.tensor_copy(mean_row[ph % 2][:].rearrange("p (g c) -> p g c", c=CG),
                                          mean.unsqueeze(2).to_broadcast([P, GROUPS, CG])
                                          ).then_inc(mean_ready, 1)
                    dve.wait_ge(means_given, asked + 2)
                    nc.vector.tensor_copy(stat_tmp[:, 2, :], num_ps[1][:, 0:GROUPS]).then_inc(log_asked, 1)
                    dve.wait_ge(log_asked, logs)
                    link(nc.vector.tensor_scalar(stat_tmp[:, 0, :], stat_tmp[:, 2, :], EPS, None, ALU.add))
                    dve.wait_ge(log_given, 2 * logs)
                    link(nc.vector.tensor_tensor(stat_tmp[:, 1, :], stat_tmp[:, 4, :], stat_tmp[:, 4, :], ALU.mult))
                    link(nc.vector.tensor_tensor(stat_tmp[:, 1, :], stat_tmp[:, 1, :], stat_tmp[:, 0, :], ALU.mult))
                    link(nc.vector.tensor_scalar(stat_tmp[:, 1, :], stat_tmp[:, 1, :], -0.5, 1.5, ALU.mult, ALU.add))
                    link(nc.vector.tensor_tensor(stat_tmp[:, 1, :], stat_tmp[:, 1, :], stat_tmp[:, 4, :], ALU.mult))
                    nc.vector.tensor_copy(rstd_row[:].rearrange("p (g c) -> p g c", c=CG),
                                          stat_tmp[:, 1, :].unsqueeze(2).to_broadcast([P, GROUPS, CG])
                                          ).then_inc(means_asked, 1)
                    dve.wait_ge(means_given, asked + 3)
                    link(nc.vector.tensor_copy(rstd_col[ph][:], den_ps[2][:, 0:C].rearrange(
                        "p (k n) -> p k n", n=P)[:, :, 0]))
                    nc.vector.tensor_tensor(rvar_col[ph][:], rstd_col[ph][:], rstd_col[ph][:], ALU.mult
                                            ).then_inc(params_ready, 1)
                    dve.wait_ge(params_ready, ph + 1)

                def approach(ph, p, par, i):
                    dve.wait_ge(recip_done, (ph * NPAIR + p) * PSEG + i + 1)
                    if i == 0 and not is_opening(ph, p, 1):
                        dve.wait_ge(ratio_done, ph * NPAIR + p)
                    nc.vector.scalar_tensor_tensor(newton[:, i, :], den_ps[i % 3][:, 0:C], TINY,
                                                   recip[par][:, i, :], ALU.add, ALU.mult).then_inc(den_used, 1)

                def weigh(ph, p, par, i):
                    dve.wait_ge(num_done, (ph * NPAIR + p) * PSEG + i + 1)
                    nc.vector.scalar_tensor_tensor(recip[par][:, i, :], num_ps[i % 2][:, 0:C], TINY,
                                                   recip[par][:, i, :], ALU.add, ALU.mult).then_inc(num_used, 1)

                def divide(ph, i, p, e):
                    slot, g = e // PAIRS, e % PAIRS
                    dve.wait_ge(num_used, (ph * NPAIR + p + 1) * PSEG)
                    dve.wait_ge(den_used, (ph * NPAIR + p + 1) * PSEG)
                    if g == 0 and not is_opening(ph, p, BODY):
                        dve.wait_ge(out_landed[slot], (ph * (TILES // 2) + i) * 16)
                    nc.vector.scalar_tensor_tensor(y_out[slot][:, g * PSEG:(g + 1) * PSEG, :], newton[:], 2.0,
                                                   recip[e % 2][:], ALU.subtract, ALU.mult).then_inc(ratio_done, 1)

                def measure_output(ph, i, lo, e):
                    q, early = e % PAIRS, e < PAIRS
                    quarter = range(q * chunk, (q + 1) * chunk)
                    layer, b = PHASES[ph]
                    if ph == 0 and lo == 0 and early:
                        if q == 0:
                            return
                        if q == 1:
                            dve.wait_ge(in_landed[3], (TILES // 4 + 1) * 16)
                        last = measure(y_out[1], range((q - 1) * chunk, GROUPS if q == 3 else q * chunk),
                                       beside_stats, 1)
                        if q == 3:
                            link(last)
                        return
                    if lo == 0 and early:
                        if ph > B:
                            return
                        tile, column, ends = ph * TILES - 1, TILES - SPLIT - 1, (PHASES[ph - 1][1], 1)
                    elif layer > 0:
                        return
                    else:
                        m = i * 2 + (-1 if early else 0)
                        tile = ph * TILES + m
                        column = m - SPLIT if lo > MID or (lo == MID and not early) else m
                        ends = (b, 0) if lo == MID and early else None
                    if q == 0:
                        dve.wait_ge(rows_out, (tile + 1) * PAIRS)
                    measure(y_out[1 if early else 0], quarter, out_stats, column).then_inc(stats_done, 1)
                    if ends:
                        dve.wait_ge(stats_done, tile * PAIRS + q + 1)
                        lane_totals(*ends, quarter, out_stats)

                def measure_beside(ph, i, lo, e, part):
                    q = e % PAIRS
                    if ph > 0 or lo >= BESIDE_END:
                        return
                    n = i * 2 + e // PAIRS
                    third = [range(GROUPS * t // 3, GROUPS * (t + 1) // 3) for t in range(3)]
                    if part == 0:
                        if lo == BESIDE_SPLIT and e < PAIRS and q < 3:
                            if q == 0:
                                dve.wait_ge(beside_done, n * 3)
                            lane_totals(1, 0, third[q], beside_stats)
                        if lo == BESIDE_END - 1 and e >= PAIRS and q > 0:
                            dve.wait_ge(beside_done, n * 3 + q)
                            lane_totals(1, 1, third[q - 1], beside_stats)
                    if q == 3:
                        return
                    if q == 0 and part == 0:
                        dve.wait_ge(beside_landed, (n + 1) * 16)
                    column = n + UPFRONT - (SPLIT if lo >= BESIDE_SPLIT else 0)
                    last = measure(beside, third[q][3 * part:3 * part + 3] if part < 2 else third[q][6:],
                                   beside_stats, column)
                    if part == 2:
                        last.then_inc(beside_done, 1)

                ask_means(0)
                finish(0)
                dve.wait_ge(in_landed[2], (TILES // 4 + 1) * 16)
                measure(y_out[0], range(GROUPS), beside_stats, 0).then_inc(tile_measured, 1)
                dve.wait_ge(tile_measured, TILES + 1)
                for ph in range(NP_):
                    def tiles(i, lo):
                        for e in range(BODY):
                            p, par = i * BODY + e, e % 2
                            approach(ph, p, par, 0)
                            approach(ph, p, par, 1)
                            weigh(ph, p, par, 0)
                            measure_beside(ph, i, lo, e, 0)
                            approach(ph, p, par, 2)
                            weigh(ph, p, par, 1)
                            measure_beside(ph, i, lo, e, 1)
                            approach(ph, p, par, 3)
                            weigh(ph, p, par, 2)
                            measure_beside(ph, i, lo, e, 2)
                            finishing = (ph + 1 < NP_ and e == BODY - 1 and lo == finish_pair(ph) // BODY - 1)
                            if finishing:
                                ask_means(ph + 1)
                            weigh(ph, p, par, 3)
                            if finishing:
                                finish(ph + 1)
                            divide(ph, i, p, e)
                            measure_output(ph, i, lo, e)
                    peeled = [0] + [MID] * (PHASES[ph][0] == 0) + [BESIDE_SPLIT, BESIDE_END - 1] * (ph == 0)
                    looped(dve, NPAIR // BODY, tiles, peeled)


def kernel(x):
    import numpy as np
    import concourse.bacc as bacc
    from concourse.bass_utils import run_bass_kernel_spmd

    nc = bacc.Bacc("TRN2", target_bir_lowering=False, num_devices=1, dynamic_dma_scratch_size=1024)
    a = np.ascontiguousarray(x)
    xin = nc.dram_tensor("in_x_dram", a.shape, mybir.dt.from_np(a.dtype), kind="ExternalInput").ap()
    out = nc.dram_tensor("out_0_dram", a.shape, mybir.dt.from_np(a.dtype), kind="ExternalOutput").ap()
    similarity_layers_kernel(nc, xin, out)
    r = run_bass_kernel_spmd(nc, [{"in_x_dram": a}], core_ids=[0])
    return r.results[0]["out_0_dram"]
```
